# Optimizing a Trainium2 kernel written in Bass

```python
import numpy as np
import jax
import jax.numpy as jnp

def _softmax(x, axis=-1):
    return jax.nn.softmax(x, axis=axis)

def _gelu(x):
    return jax.nn.gelu(x, approximate=True)

def _silu(x):
    return jax.nn.silu(x)

def _sigmoid(x):
    return jax.nn.sigmoid(x)

def _layernorm(x, axis=-1, eps=1e-05):
    m = jnp.mean(x, axis=axis, keepdims=True)
    v = jnp.var(x, axis=axis, keepdims=True)
    return (x - m) / jnp.sqrt(v + eps)

def _scatter_add(tgt, idx, src, axis=0):
    return tgt.at[idx].add(src)

def _segment_sum(src, seg, n):
    return jax.ops.segment_sum(src, seg, n)
kernel_name = 'mk_seq_postln_d1_jaxref_r8_b52411'

def setup_inputs(seed: int=0):
    np.random.seed(seed)
    _w = jnp.asarray

    def _L0_attn_setup():
        import jax, jax.numpy as jnp
        import numpy as np
        D_MODEL = 128
        NUM_HEADS = 16
        D_K = D_MODEL // NUM_HEADS
        THETA = 10000.0

        def _rope(x, positions):
            d = x.shape[-1]
            inv_freq = THETA ** (-jnp.arange(0, d, 2, dtype=jnp.float32) / d)
            ang = positions[:, :, None].astype(jnp.float32) * inv_freq[None, None, :]
            cos = jnp.cos(ang)[:, None, :, :]
            sin = jnp.sin(ang)[:, None, :, :]
            x1 = x[..., 0::2]
            x2 = x[..., 1::2]
            r1 = x1 * cos - x2 * sin
            r2 = x1 * sin + x2 * cos
            out = jnp.stack([r1, r2], axis=-1).reshape(x.shape)
            return out
        key = jax.random.key(seed)
        k1, k2, k3 = jax.random.split(key, 3)
        B, S = (4, 256)
        x = jax.random.normal(k1, (B, S, D_MODEL), dtype=jnp.float32)
        W_qkv = jax.random.normal(k2, (3 * D_MODEL, D_MODEL), dtype=jnp.float32) * (1.0 / np.sqrt(D_MODEL))
        W_o = jax.random.normal(k3, (D_MODEL, D_MODEL), dtype=jnp.float32) * (1.0 / np.sqrt(D_MODEL))
        return {'x': x, 'W_qkv': W_qkv, 'W_o': W_o}
    _L0_attn_in = _L0_attn_setup()

    def _L0_ffn_setup():
        import jax, jax.numpy as jnp
        import numpy as np
        INT4_QMAX = 7.0

        def simulate_quantize_int4(w):
            scale = jnp.max(jnp.abs(w)) / INT4_QMAX
            q = jnp.clip(jnp.round(w / scale), -8.0, 7.0)
            return q * scale
        key = jax.random.key(seed)
        k_x, k_w, k_bias, k_a, k_b = jax.random.split(key, 5)
        d_in, features, rank = (128, 128, 16)
        x = jax.random.normal(k_x, (4, 1024, d_in), dtype=jnp.float32)
        kernel = jax.random.normal(k_w, (d_in, features), dtype=jnp.float32)
        bias = jax.random.normal(k_bias, (features,), dtype=jnp.float32)
        a = jax.random.normal(k_a, (d_in, rank), dtype=jnp.float32) * (1.0 / np.sqrt(d_in))
        b = jax.random.normal(k_b, (rank, features), dtype=jnp.float32) * 0.01
        return {'x': x, 'kernel': kernel, 'bias': bias, 'a': a, 'b': b}
    _L0_ffn_in = _L0_ffn_setup()
    _d = {'L0_attn_x': _L0_attn_in['x'], 'L0_attn_W_qkv': _L0_attn_in['W_qkv'], 'L0_attn_W_o': _L0_attn_in['W_o'], 'L0_ffn_kernel': _L0_ffn_in['kernel'], 'L0_ffn_bias': _L0_ffn_in['bias'], 'L0_ffn_a': _L0_ffn_in['a'], 'L0_ffn_b': _L0_ffn_in['b']}
    _x0 = _d['L0_attn_x']
    _d['L0_attn_x'] = jax.random.normal(jax.random.fold_in(jax.random.key(seed), 1), (1, 2048, 128), dtype=_x0.dtype)
    del _x0
    return _d

def reference(L0_attn_x, L0_attn_W_qkv, L0_attn_W_o, L0_ffn_kernel, L0_ffn_bias, L0_ffn_a, L0_ffn_b):

    def _L0_attn_ref(x, W_qkv, W_o):
        import jax, jax.numpy as jnp
        import numpy as np
        D_MODEL = 128
        NUM_HEADS = 16
        D_K = D_MODEL // NUM_HEADS
        THETA = 10000.0

        def _rope(x, positions):
            d = x.shape[-1]
            inv_freq = THETA ** (-jnp.arange(0, d, 2, dtype=jnp.float32) / d)
            ang = positions[:, :, None].astype(jnp.float32) * inv_freq[None, None, :]
            cos = jnp.cos(ang)[:, None, :, :]
            sin = jnp.sin(ang)[:, None, :, :]
            x1 = x[..., 0::2]
            x2 = x[..., 1::2]
            r1 = x1 * cos - x2 * sin
            r2 = x1 * sin + x2 * cos
            out = jnp.stack([r1, r2], axis=-1).reshape(x.shape)
            return out
        B, S, _ = x.shape
        H, dk = (NUM_HEADS, D_K)
        qkv = jnp.einsum('bsd,ed->bse', x, W_qkv)
        qkv = qkv.reshape(B, S, 3, H, dk).transpose(2, 0, 3, 1, 4)
        q, k, v = (qkv[0], qkv[1], qkv[2])
        positions = jnp.broadcast_to(jnp.arange(S)[None, :], (B, S))
        q = _rope(q, positions)
        k = _rope(k, positions)
        scores = jnp.einsum('bhqd,bhkd->bhqk', q, k) / jnp.sqrt(jnp.float32(dk))
        causal = jnp.tril(jnp.ones((S, S), dtype=bool))
        scores = jnp.where(causal[None, None, :, :], scores, -jnp.inf)
        attn = jax.nn.softmax(scores, axis=-1)
        out = jnp.einsum('bhqk,bhkd->bhqd', attn, v)
        out = out.transpose(0, 2, 1, 3).reshape(B, S, H * dk)
        return jnp.einsum('bsd,ed->bse', out, W_o)

    def _L0_ffn_ref(x, kernel, bias, a, b):
        import jax, jax.numpy as jnp
        import numpy as np
        INT4_QMAX = 7.0

        def simulate_quantize_int4(w):
            scale = jnp.max(jnp.abs(w)) / INT4_QMAX
            q = jnp.clip(jnp.round(w / scale), -8.0, 7.0)
            return q * scale
        w = simulate_quantize_int4(kernel)
        y = jnp.einsum('bsd,df->bsf', x, w) + bias
        lora = jnp.einsum('bsr,rf->bsf', jnp.einsum('bsd,dr->bsr', x, a), b)
        return y + lora
    x = L0_attn_x
    x = _layernorm(x + _L0_attn_ref(x, L0_attn_W_qkv, L0_attn_W_o), axis=-1)
    x = _layernorm(x + _L0_ffn_ref(x, L0_ffn_kernel, L0_ffn_bias, L0_ffn_a, L0_ffn_b), axis=-1)
    return x

_drawn_inputs = setup_inputs


def setup_inputs(seed=0):
    import zlib

    import numpy as np

    out = dict(_drawn_inputs(seed))
    spreads = {}
    factors = {'L0_ffn_a': 8.0, 'L0_ffn_b': 8.0}
    for name, (base, spread) in spreads.items():
        noise = np.random.default_rng([zlib.crc32(name.encode()), seed]).standard_normal(out[name].shape)
        drawn = base * np.exp(spread * noise) if base else spread * noise
        out[name] = jnp.asarray(drawn.astype(out[name].dtype))
    for name, factor in factors.items():
        out[name] = (out[name] * factor).astype(out[name].dtype)
    return out
```

```python
import numpy as np
import concourse.bass as bass
from concourse import mybir
from contextlib import ExitStack

S, D, H, DK = 2048, 128, 16, 8
RANK = 16
THETA = 10000.0
TOK = 128
CH = 512
NT, NC, TPC = S // TOK, S // CH, CH // TOK
HG = 4
NG = H // HG
PARTS = 3
TERMS = PARTS * PARTS * DK
SHIFT_ROW = 96
KROWS = 128
VW = 32
PRING = 4
NEG = -3.0e38
EPS = 1e-5
ONE_PAIR = 1.0 + 0x3F80 / 2 ** 23


def rope_tables():
    inv = np.float32(THETA) ** (-np.arange(0, DK, 2, dtype=np.float32) / np.float32(DK))
    ang = np.arange(S, dtype=np.float32)[None, :] * inv.astype(np.float32)[:, None]
    cos = np.repeat(np.cos(ang), 2, axis=0)
    sin = np.repeat(np.sin(ang), 2, axis=0)
    sin[0::2] *= -1
    rows = [np.tile(np.repeat(t, HG, axis=0), (NG, 1)) for t in (cos, sin)]
    return np.ascontiguousarray(np.stack(rows).astype(np.float32))


def score_units(c):
    return [(kk, ii, hp) for kk in range(c + 1) for ii in range(TPC) for hp in range(HG // 2)]


def schedule(last):
    steps = [(c, j) for c in range(NC) for j in range(TPC * (c + 1))]
    here = [("A", 0, 2, u) for u in score_units(2)]
    third = [("A", 0, 3, u) for u in score_units(3)]
    here += third[:2] + [("N", 0, 2)] + third[2:7] + [("M", 0, 2)] + third[7:] + [("N", 0, 3)]
    nxt = []
    if not last:
        one = [("A", 1, 1, u) for u in score_units(1)]
        nxt = [("A", 1, 0, u) for u in score_units(0)] + one[:2] + [("N", 1, 0)] + one[2:7] + [("M", 1, 0)] + one[7:] + [("N", 1, 1)]
    m_here = here.index(("M", 0, 2)) + 1
    n_early, n_here, n_next = 11, 22, 14
    post = {}
    if last:
        for c in range(NC - 1):
            first = sum(TPC * (b + 1) for b in range(c + 1))
            for k, at in enumerate((3, 3, 4, 5, 6, 7) if c == 0 else (3, 4, 5, 6, 8, 9)):
                post.setdefault(first + at, []).append(("POST", c, k))
    out, done_h, done_n, pv = [], 0, 0, []
    for J, (c, j) in enumerate(steps):
        out.append(("S", c, j, 0))
        if len(pv) > 1:
            out.append(("PV",) + pv.pop(0))
        out.append(("S", c, j, 1))
        pv.append((c, j))
        if J < 24:
            upto = ((J + 1) * m_here // n_early if J < n_early else
                    min(len(here), m_here + (J + 1 - n_early) * (len(here) - m_here) // (n_here - n_early)))
            out += here[done_h:upto]
            done_h = upto
            if J == 23:
                out.append(("M", 0, 3))
        elif nxt:
            upto = min(len(nxt), (J - 23) * len(nxt) // n_next)
            out += nxt[done_n:upto]
            done_n = upto
        out += post.get(J, [])
    out.append(("PV",) + pv.pop(0))
    if not last:
        out.append(("M", 1, 1))
    out.append(("PV",) + pv.pop(0))
    if last:
        out += [("POST", NC - 1, k) for k in range(6)]
    return out


RING_EVENTS = ("A", "M", "POST")
PRO_UNITS = len(score_units(0)) + len(score_units(1)) + 2
RING_0 = PRO_UNITS + 1
GROUP_UNITS = sum(e[0] in RING_EVENTS for e in schedule(False))
STEPS = sum(TPC * (c + 1) for c in range(NC))
BLOCKS = STEPS * HG


def step_index(c, j):
    return sum(TPC * (b + 1) for b in range(c)) + j


def attention_block(nc, x, w_qkv, w_o, ffn_w, ffn_bias, lora_a, lora_b, tables, out):
    fp32, bf16 = mybir.dt.float32, mybir.dt.bfloat16
    ALU, ACT, AX = mybir.AluOpType, mybir.ActivationFunctionType, mybir.AxisListType
    absmax = bass.bass_isa.ReduceOp.absmax

    x_t = x.rearrange("a (t p) d -> p (a t) d", p=TOK)
    out_t = out.rearrange("a (t p) d -> p (a t) d", p=TOK)

    ctx = ExitStack()
    with ctx:
        def sb(name, shape, dt=fp32):
            return ctx.enter_context(nc.sbuf_tensor(name, shape, dt))

        def sem(name):
            return ctx.enter_context(nc.semaphore(name))

        x_sb = sb("x_sb", [128, NT, D])
        wqkv_sb = sb("wqkv_sb", [128, 3, D])
        wo_sb = sb("wo_sb", [128, D])
        ffn_sb = sb("ffn_sb", [128, D])
        a_sb = sb("a_sb", [128, RANK])
        b_sb = sb("b_sb", [RANK, D])
        bias_sb = sb("bias_sb", [128, D])
        ident = sb("ident", [128, 128])
        ident_h = sb("ident_h", [128, 128], bf16)
        causal = sb("causal", [128, 128], bf16)
        wT = sb("wT", [128, 4, D])
        wTs = sb("wTs", [128, 2, D])
        aT = sb("aT", [RANK, 128])
        ffn_q = sb("ffn_q", [128, D])
        wst = sb("wst", [128, 8])
        rot = sb("rot", [128, 2, 3, CH])
        qp = sb("qp", [128, 2, PARTS, CH], bf16)
        kp = sb("kp", [128, 2, PARTS, CH], bf16)
        q_dram = nc.dram_tensor("q_parts", [NG, NC, PARTS, DK * HG, CH], bf16, kind="Internal").ap()
        k_dram = nc.dram_tensor("k_parts", [NG, NC, PARTS, DK * HG, CH], bf16, kind="Internal").ap()
        v_all = sb("v_all", [128, NT, H, DK])
        qA = sb("qA", [128, NC, HG, CH], bf16)
        kA = sb("kA", [128, NC, HG, CH], bf16)
        qB = sb("qB", [128, NC, HG, CH], bf16)
        kB = sb("kB", [128, NC, HG, CH], bf16)
        v_g = sb("v_g", [128, NT, HG, VW])
        pmax = sb("pmax", [128, NC, HG, TPC, NC])
        nmax = sb("nmax", [128, NC, HG * TPC])
        nrest = sb("nrest", [128, NC, HG * TPC])
        nparts = sb("nparts", [128, NC, 128], bf16)
        mrows = sb("mrows", [PARTS * HG * TPC, NC, TOK], bf16)
        probs = sb("probs", [128, PRING, HG, CH])
        xT = probs[:, 0, 0:2, :]
        cs_sb = probs[:, 1, :, :].rearrange("p (b w) s -> p b w s", w=2)
        oT = sb("oT", [128, NG, S])
        rsum = sb("rsum", [128, TPC, H])
        on, res, x1 = (rot[:, 0, i, :].rearrange("p (t d) -> p t d", d=D) for i in range(3))
        onT, x1T = rot[:, 1, 0, :], rot[:, 1, 1, :]
        x1b = rot[:, 1, 2, :].rearrange("p (t d) -> p t d", d=D)
        stats = sb("stats", [128, TPC, 6])
        mv = sb("mv", [128, TPC, 2])
        rstd = sb("rstd", [128, TPC])
        mhalf = sb("mhalf", [128, TPC])
        y_sb = sb("y_sb", [128, TPC, D])

        ring = ctx.enter_context(nc.psum_tensor("ring", [128, 2, 2, CH], fp32))
        sT = ctx.enter_context(nc.psum_tensor("sT", [128, 2, CH], fp32))
        oP = ctx.enter_context(nc.psum_tensor("oP", [128, 2, CH], fp32))
        prep_bank = [sT[:, 0, :], sT[:, 1, :], oP[:, 0, :], oP[:, 1, :]]

        ld_w = sem("ld_w")
        ld_ffn = sem("ld_ffn")
        ld_x = [sem(f"ld_x{c}") for c in range(NC)]
        ld_cs = [sem(f"ld_cs{c}") for c in range(NC)]
        consts = sem("consts")
        filled = sem("filled")
        filled_b = sem("filled_b")
        bank_done = [sem(f"bank_done{b}") for b in range(4)]
        bank_free = [sem(f"bank_free{b}") for b in range(4)]
        rope_sum = sem("rope_sum")
        part_done = sem("part_done")
        rest_done = sem("rest_done")
        w_done = sem("w_done")
        wq_step = sem("wq_step")
        parts_out = [sem(f"parts_out{c}") for c in range(NC)]
        qkA_in = [sem(f"qkA_in{c}") for c in range(NC)]
        qkB_in = [sem(f"qkB_in{c}") for c in range(NC)]
        unit_done = sem("unit_done")
        unit_free = sem("unit_free")
        nmax_done = sem("nmax_done")
        nsplit = sem("nsplit")
        mrow_in = [sem(f"mrow_in{c}") for c in range(NC)]
        s_done = sem("s_done")
        exp_done = sem("exp_done")
        masked = sem("masked")
        gate = sem("gate")
        probs_free = sem("probs_free")
        o_free = sem("o_free")
        v_staged = sem("v_staged")
        dve_post = sem("dve_post")
        pool_post = sem("pool_post")
        stored = sem("stored")

        block = ctx.enter_context(nc.Block())

        def groups(eng, body):
            with eng.Fori(0, NG - 1) as g:
                body(g, False)
            body(NG - 1, True)

        PREP = [("W", 0), ("L", 0)]
        for c in range(NC):
            PREP += [(k, c) for k in ("X", "Q", "QS", "K", "KS", "V")]
        PREP_AT = {u: n for n, u in enumerate(PREP)}

        def prep_bank_of(u):
            return PREP_AT[u] % 4, PREP_AT[u] // 4 + 1

        def prep_begin(pe, u):
            b, n = prep_bank_of(u)
            if n > 1:
                pe.wait_ge(bank_free[b], n - 1)
            return prep_bank[b]

        def prep_read(eng, u):
            b, n = prep_bank_of(u)
            eng.wait_ge(bank_done[b], n)
            return prep_bank[b]

        def store_parts(sp, c):
            for a in range(PARTS):
                for parts, dram in ((qp, q_dram), (kp, k_dram)):
                    sp.dma_start(dram[:, c, a, :, :], parts[:, c % 2, a, :]).then_inc(parts_out[c], 16)

        N_A = PARTS + 1

        def load_A(sp, c, g):
            for a in range(PARTS):
                sp.dma_start(qA[a * PARTS * DK:(a + 1) * PARTS * DK, c, :, :].rearrange("r h s -> r (h s)"),
                             q_dram[bass.ds(g, 1), c, a, :, :].rearrange("x (d h) s -> x d (h s)", h=HG)
                             .to_broadcast([PARTS, DK, HG * CH])).then_inc(qkA_in[c], 16)
            sp.dma_start(kA[0:TERMS, c, :, :].rearrange("r h s -> r (h s)"),
                         k_dram[bass.ds(g, 1), c, :, :, :].rearrange("x b (d h) s -> x (b d) (h s)", h=HG)
                         .to_broadcast([PARTS, PARTS * DK, HG * CH])).then_inc(qkA_in[c], 16)

        def load_B(sp, c):
            sp.dma_start(qB[0:TERMS, c, :, :], qA[0:TERMS, c, :, :]).then_inc(qkB_in[c], 16)
            sp.dma_start(kB[0:TERMS, c, :, :], kA[0:TERMS, c, :, :]).then_inc(qkB_in[c], 16)

        def load_maxima(sp, c, u_free):
            sp.wait_ge(unit_free, u_free)
            for a in range(PARTS):
                sp.dma_start(qB[SHIFT_ROW + a:SHIFT_ROW + a + 1, c, :, :],
                             mrows[a * HG * TPC:(a + 1) * HG * TPC, c, :]).then_inc(mrow_in[c], 16)

        POOL_1 = 2 + 2 * TPC
        POOL_2 = 2 + TPC

        def post_pool_count(c, norm):
            return c * (POOL_1 + POOL_2) + POOL_1 + (POOL_2 if norm else 0)

        DVE_ON = 2 * TPC - 2
        DVE_POST = DVE_ON + 2 * (2 * TPC)

        @block.sync
        def _(sp):
            sp.dma_start(x_sb[:, 0:TPC, :], x_t[:, 0:TPC, :]).then_inc(ld_x[0], 16)
            sp.dma_start(wqkv_sb[:, :, :], w_qkv.rearrange("(k p) d -> p k d", p=128)).then_inc(ld_w, 16)
            sp.dma_start(wo_sb[:, :], w_o).then_inc(ld_w, 16)
            sp.dma_start(a_sb[:, :], lora_a).then_inc(ld_w, 16)
            for c in range(2):
                sp.dma_start(cs_sb[:, c, :, :],
                             tables[:, :, c * CH:(c + 1) * CH].rearrange("w p s -> p w s")).then_inc(ld_cs[c], 16)
            for c in range(1, NC):
                sp.dma_start(x_sb[:, c * TPC:(c + 1) * TPC, :], x_t[:, c * TPC:(c + 1) * TPC, :]).then_inc(ld_x[c], 16)
            sp.dma_start(ffn_sb[:, :], ffn_w).then_inc(ld_ffn, 16)
            sp.dma_start(b_sb[:, :], lora_b).then_inc(ld_ffn, 16)
            sp.dma_start(bias_sb[:, :], ffn_bias.rearrange("(a n) -> a n", a=1).to_broadcast([128, D])).then_inc(ld_ffn, 16)
            sp.wait_ge(filled, 3)
            sp.wait_ge(filled_b, 2)
            for c in range(NC):
                sp.wait_ge(part_done, 4 * (c + 1))
                sp.wait_ge(rest_done, 4 * (c + 1))
                store_parts(sp, c)
                sp.wait_ge(parts_out[c], 16 * 2 * PARTS)
                load_A(sp, c, 0)
                if c + 2 < NC:
                    sp.dma_start(cs_sb[:, c % 2, :, :],
                                 tables[:, :, (c + 2) * CH:(c + 3) * CH].rearrange("w p s -> p w s")).then_inc(ld_cs[c + 2], 16)
                sp.wait_ge(qkA_in[c], 16 * N_A)
                load_B(sp, c)
            u = 0
            for c in range(2):
                u += len(score_units(c)) + 1
                load_maxima(sp, c, 2 + u)

            def body(g, last):
                u = 0
                for e in schedule(last):
                    u += e[0] in RING_EVENTS
                    if e[0] == "M":
                        load_maxima(sp, e[2], g * GROUP_UNITS + (2 + RING_0 + u))
                    if e[0] == "A" and not last and e[2] == 3 and e[3][1:] == (TPC - 1, HG // 2 - 1):
                        sp.wait_ge(unit_done, g * GROUP_UNITS + (RING_0 + u))
                        sp.wait_ge(qkB_in[e[3][0]], g * 32 + 32)
                        load_A(sp, e[3][0], g + 1)
                    if e[0] == "S" and not last and e[1] == NC - 1 and e[3] == 1 and e[2] % TPC == TPC - 1:
                        c = e[2] // TPC
                        sp.wait_ge(s_done, g * BLOCKS + (step_index(NC - 1, e[2]) + 1) * HG)
                        sp.wait_ge(qkA_in[c], g * 16 * N_A + 2 * 16 * N_A)
                        load_B(sp, c)

            groups(sp, body)
            for c in range(NC):
                sp.wait_ge(pool_post, post_pool_count(c, 1))
                sp.dma_start(out_t[:, c * TPC:(c + 1) * TPC, :], y_sb[:, :, :]).then_inc(stored, 16)
            sp.wait_ge(stored, 16 * NC)

        def stage_v(pool, c, g):
            tiles = slice(c * TPC, (c + 1) * TPC)
            nc.gpsimd.tensor_copy(v_g[:, tiles, :, 0:DK], v_all[:, tiles, bass.ds(g * HG, HG), :]).then_inc(v_staged, 1)

        def split_maxima(pool, c, before, n):
            n_m = HG * TPC
            part = [nparts[:, c, a * n_m:(a + 1) * n_m] for a in range(PARTS)]
            pool.wait_ge(nmax_done, before + n)
            pool.sem_inc(gate, 1)
            nc.gpsimd.tensor_copy(part[0], nmax[:, c, :]).then_inc(nsplit, 1)
            pool.wait_ge(nsplit, before * 4 + (4 * n - 3))
            nc.gpsimd.tensor_tensor(nrest[:, c, :], nmax[:, c, :], part[0], ALU.subtract).then_inc(nsplit, 1)
            pool.wait_ge(nsplit, before * 4 + (4 * n - 2))
            pool.sem_inc(gate, 1)
            nc.gpsimd.tensor_copy(part[1], nrest[:, c, :]).then_inc(nsplit, 1)
            pool.wait_ge(nsplit, before * 4 + (4 * n - 1))
            nc.gpsimd.tensor_tensor(part[2], nrest[:, c, :], part[1], ALU.subtract).then_inc(nsplit, 1)

        def post_norm(pool, c, second):
            base = post_pool_count(c, second) - (POOL_2 if second else POOL_1)
            pool.wait_ge(dve_post, DVE_POST * c + (DVE_POST if second else DVE_ON + 2 * TPC))
            nc.gpsimd.tensor_scalar(rstd[:, :], mv[:, :, 1], EPS, None, ALU.add).then_inc(pool_post, 1)
            pool.wait_ge(pool_post, base + 1)
            nc.gpsimd.tensor_tensor(rstd[:, :], rstd[:, :], mhalf[:, :], ALU.pow).then_inc(pool_post, 1)
            pool.wait_ge(pool_post, base + 2)
            if second and c > 0:
                pool.wait_ge(stored, 16 * c)
            for t in range(TPC):
                nc.gpsimd.tensor_scalar((y_sb if second else x1)[:, t, :], res[:, t, :], mv[:, t, 0:1], rstd[:, t:t + 1],
                                        ALU.subtract, ALU.mult).then_inc(pool_post, 1)
            if not second:
                for t in range(TPC):
                    pool.wait_ge(pool_post, base + 3 + t)
                    nc.gpsimd.tensor_tensor(x1b[:, t, :], x1[:, t, :], bias_sb[:, :], ALU.add).then_inc(pool_post, 1)

        @block.gpsimd
        def _(pool):
            pool.memset(ident[:, :], 0.0).then_inc(consts, 1)
            pool.memset(ident_h[:, :], 0.0).then_inc(consts, 1)
            pool.memset(causal[:, :], 0.0).then_inc(consts, 1)
            pool.wait_ge(consts, 3)
            for m in (ident, ident_h):
                pool.affine_select(out=m[:, :], in_=m[:, :], compare_op=ALU.not_equal, fill=1.0, base=0,
                                   pattern=[[-1, 128]], channel_multiplier=1).then_inc(consts, 1)
            pool.affine_select(out=causal[:, :], in_=causal[:, :], compare_op=ALU.is_ge, fill=NEG, base=0,
                               pattern=[[-1, 128]], channel_multiplier=1).then_inc(consts, 1)
            pool.wait_ge(ld_ffn, 48)
            pool.wait_ge(wq_step, 1)
            nc.gpsimd.partition_all_reduce(wst[:, 1:2], wst[:, 0:1], 128, absmax).then_inc(wq_step, 1)
            for n, (o, a, k, b, op) in enumerate(((2, 1, 1.0 / 7.0, None, None), (4, 2, 8.0, 1, ALU.subtract), (4, 2, 1.0, 4, ALU.subtract),
                                                  (4, 4, 1.0 / 7.0, 2, ALU.add))):
                pool.wait_ge(wq_step, n + 2)
                if b is None:
                    nc.gpsimd.tensor_scalar(wst[:, o:o + 1], wst[:, a:a + 1], k, None, ALU.mult).then_inc(wq_step, 1)
                else:
                    nc.gpsimd.tensor_scalar(wst[:, o:o + 1], wst[:, a:a + 1], k, wst[:, b:b + 1], ALU.mult, op).then_inc(wq_step, 1)
            pool.wait_ge(wq_step, 6)
            pool.memset(kB[64:96, :, :, :].bitcast(fp32), 0.0).then_inc(filled_b, 1)
            pool.wait_ge(filled_b, 1)
            pool.memset(kB[96:128, :, :, :].bitcast(fp32), ONE_PAIR).then_inc(filled_b, 1)
            pool.wait_ge(filled_b, 2)
            pool.memset(v_g[:, :, :, :], 0.0).then_inc(v_staged, 1)
            pool.wait_ge(v_staged, 1)
            pool.memset(v_g[:, :, :, DK:DK + 1], 1.0).then_inc(v_staged, 1)
            pool.memset(mhalf[:, :], -0.5).then_inc(v_staged, 1)
            pool.memset(nparts[:, :, :], 0.0).then_inc(v_staged, 1)
            for c in range(NC):
                for w, parts in ((0, qp), (1, kp)):
                    n = 2 * c + w
                    for kind in (("Q", "QS"), ("K", "KS"))[w]:
                        b, uses = prep_bank_of((kind, c))
                        pool.wait_ge(bank_free[b], uses)
                    nc.gpsimd.tensor_tensor(rot[:, w, 2, :], rot[:, w, 0, :], rot[:, w, 1, :], ALU.add).then_inc(rope_sum, 1)
                    pool.wait_ge(rope_sum, n + 1)
                    pool.wait_ge(part_done, 2 * n + 1)
                    nc.gpsimd.tensor_tensor(rot[:, w, 2, :], rot[:, w, 2, :], parts[:, c % 2, 0, :], ALU.subtract).then_inc(rest_done, 1)
                    pool.wait_ge(rest_done, 2 * n + 1)
                    pool.wait_ge(part_done, 2 * n + 2)
                    nc.gpsimd.tensor_tensor(parts[:, c % 2, 2, :], rot[:, w, 2, :], parts[:, c % 2, 1, :], ALU.subtract).then_inc(rest_done, 1)
                b, uses = prep_bank_of(("V", c))
                pool.wait_ge(bank_free[b], uses)
                pool.wait_ge(v_staged, 4)
                stage_v(pool, c, 0)
            for c in range(2):
                split_maxima(pool, c, 0, c + 1)

            def body(g, last):
                n_split = 2
                for e in schedule(last):
                    if e[0] == "S" and e[3] == 1 and e[2] >= TPC * e[1]:
                        c, jj = e[1], e[2] - TPC * e[1]
                        J = step_index(c, e[2])
                        pool.wait_ge(exp_done, g * BLOCKS + (2 + (J + 1) * HG))
                        pool.sem_inc(gate, 1)
                        p = probs[:, J % PRING, :, jj * TOK:(jj + 1) * TOK]
                        pool.affine_select(out=p, in_=p, compare_op=ALU.is_ge, fill=0.0, base=0,
                                           pattern=[[0, HG], [1, TOK]], channel_multiplier=-1).then_inc(masked, 1)
                    if e[0] == "N":
                        n_split = n_split + 1
                        split_maxima(pool, e[2], g * 4, n_split)
                    if e[0] == "PV" and not last and e[1] == NC - 1 and e[2] % TPC == TPC - 1:
                        c = e[2] // TPC
                        pool.wait_ge(probs_free, g * STEPS + (PRING + step_index(NC - 1, e[2]) + 1))
                        pool.sem_inc(gate, 1)
                        stage_v(pool, c, g + 1)
                    if e[0] == "POST" and e[2] in (3, 5):
                        post_norm(pool, e[1], 0 if e[2] == 3 else 1)

            groups(pool, body)

        @block.scalar
        def _(act):
            def evac(u, dst, src_of, done=None):
                src = prep_read(act, u)
                ins = nc.scalar.copy(dst, src_of(src))
                ins.then_inc(bank_free[prep_bank_of(u)[0]], 1)

            src = prep_read(act, ("W", 0))
            for w in range(2):
                nc.scalar.copy(wT[:, w, :].rearrange("p (g d h) -> p g h d", g=NG, d=DK),
                               src[:, w * D:(w + 1) * D].rearrange("p (g h d) -> p g h d", g=NG, d=DK)).then_inc(w_done, 1)
            nc.scalar.copy(wT[:, 2:4, :], src[:, 2 * D:4 * D].rearrange("p (w d) -> p w d", w=2)).then_inc(bank_free[0], 1)
            act.wait_ge(w_done, 2)
            for w in range(2):
                src = wT[:, w, :].rearrange("p (n e h) -> p n e h", e=2, h=HG)
                dst = wTs[:, w, :].rearrange("p (n e h) -> p n e h", e=2, h=HG)
                for e in range(2):
                    nc.scalar.copy(dst[:, :, e, :], src[:, :, 1 - e, :]).then_inc(w_done, 1)
            evac(("L", 0), aT[:, :], lambda s: s[0:RANK, 0:128])
            for c in range(NC):
                evac(("X", c), xT[:, c % 2, :], lambda s: s)
                if c >= 2:
                    act.wait_ge(parts_out[c - 2], 16 * 2 * PARTS)
                for w, parts in ((0, qp), (1, kp)):
                    n = 2 * c + w
                    act.wait_ge(rope_sum, n + 1)
                    nc.scalar.copy(parts[:, c % 2, 0, :], rot[:, w, 2, :]).then_inc(part_done, 1)
                    act.wait_ge(rest_done, 2 * n + 1)
                    nc.scalar.copy(parts[:, c % 2, 1, :], rot[:, w, 2, :]).then_inc(part_done, 1)
                src = prep_read(act, ("V", c))
                b = prep_bank_of(("V", c))[0]
                nc.scalar.copy(v_all[:, c * TPC:(c + 1) * TPC, :, :],
                               src.rearrange("p (t h d) -> p t h d", t=TPC, h=H)).then_inc(bank_free[b], 1)
            act.sem_inc(exp_done, 2)
            act.sem_inc(o_free, 2)

            def flush_o(g, c):
                act.wait_ge(probs_free, g * STEPS + (PRING + step_index(c, TPC * (c + 1) - 1) + 1))
                nc.scalar.copy(oT[:, bass.ds(g, 1), c * CH:(c + 1) * CH],
                               oP[:, c % 2, :].rearrange("p (a s) -> p a s", a=1)).then_inc(o_free, 1)

            def body(g, last):
                evac_o = []
                for e in schedule(last):
                    if e[0] == "S":
                        c, j = e[1], e[2]
                        J = step_index(c, j)
                        lo = max(0, j - TPC * c) * TOK
                        act.wait_ge(probs_free, g * STEPS + (J + 1))
                        for h in (2 * e[3], 2 * e[3] + 1):
                            act.wait_ge(s_done, g * BLOCKS + (J * HG + h + 1))
                            nc.scalar.activation(probs[:, J % PRING, h, lo:CH], sT[:, h % 2, lo:CH], ACT.Exp,
                                                 scale=float(DK) ** -0.5).then_inc(exp_done, 1)
                        if e[3] == 1 and evac_o:
                            flush_o(g, evac_o.pop())
                    if e[0] == "PV" and e[2] == TPC * (e[1] + 1) - 1:
                        evac_o.append(e[1])
                        if e[1] == NC - 1:
                            flush_o(g, evac_o.pop())

            groups(act, body)

        @block.vector
        def _(dve):
            nc.vector.memset(qA[64:128, :, :, :].bitcast(fp32), 0.0).then_inc(filled, 1)
            nc.vector.memset(kA[64:128, :, :, :].bitcast(fp32), 0.0).then_inc(filled, 1)
            nc.vector.memset(qB[64:128, :, :, :].bitcast(fp32), 0.0).then_inc(filled, 1)
            dve.wait_ge(ld_ffn, 48)
            nc.vector.tensor_reduce(wst[:, 0:1], ffn_sb[:, :], AX.X, ALU.max, apply_absolute_value=True).then_inc(wq_step, 1)
            for c in range(NC):
                dve.wait_ge(ld_cs[c], 16)
                for w, names in ((0, ("Q", "QS")), (1, ("K", "KS"))):
                    if c > 0:
                        dve.wait_ge(rest_done, 4 * (c - 1) + 2 * w + 2)
                        dve.wait_ge(part_done, 4 * (c - 1) + 2 * w + 2)
                    for i, kind in enumerate(names):
                        src = prep_read(dve, (kind, c))
                        b = prep_bank_of((kind, c))[0]
                        nc.vector.tensor_tensor(rot[:, w, i, :], src, cs_sb[:, c % 2, i, :], ALU.mult).then_inc(bank_free[b], 1)
            dve.sem_inc(unit_free, 2)

            def row_max(c, unit, slot, u):
                kk, ii, hp = unit
                w = CH if kk < c else (ii + 1) * TOK
                dve.wait_ge(unit_done, u)
                nc.vector.tensor_reduce(pmax[:, c, 2 * hp:2 * hp + 2, ii, kk], ring[:, slot, :, 0:w],
                                        AX.X, ALU.max).then_inc(unit_free, 1)

            def combine(c, u):
                dve.wait_ge(unit_free, 2 + u)
                nc.vector.tensor_reduce(nmax[:, c, :], pmax[:, c, :, :, 0:c + 1].rearrange("p h i k -> p (h i) k"),
                                        AX.X, ALU.max, negate=True).then_inc(nmax_done, 1)

            def rows(c, slot, u):
                dve.wait_ge(unit_done, u)
                nc.vector.tensor_copy(mrows[:, c, :], ring[0:PARTS * HG * TPC, slot, 0, 0:TOK // 2].bitcast(bf16)).then_inc(unit_free, 1)

            u = 0
            for c in range(2):
                for unit in score_units(c):
                    row_max(c, unit, u % 2, u + 1)
                    u += 1
                combine(c, u)
                rows(c, u % 2, u + 1)
                u += 1
            dve.wait_ge(wq_step, 6)
            nc.vector.reciprocal(wst[:, 3:4], wst[:, 4:5]).then_inc(wq_step, 1)
            dve.wait_ge(wq_step, 7)
            nc.vector.tensor_scalar(ffn_q[:, :], ffn_sb[:, :], wst[:, 3:4], None, ALU.mult).then_inc(wq_step, 1)
            dve.wait_ge(wq_step, 8)
            nc.vector.tensor_scalar(ffn_q[:, :], ffn_q[:, :], 12582912.0, 12582912.0, ALU.add, ALU.subtract).then_inc(wq_step, 1)
            dve.wait_ge(wq_step, 9)
            nc.vector.tensor_scalar(ffn_q[:, :], ffn_q[:, :], -8.0, 7.0, ALU.max, ALU.min).then_inc(wq_step, 1)
            dve.wait_ge(wq_step, 10)
            nc.vector.tensor_scalar(ffn_q[:, :], ffn_q[:, :], wst[:, 4:5], None, ALU.mult).then_inc(wq_step, 1)
            dve.wait_ge(wq_step, 11)
            dve.wait_ge(unit_done, PRO_UNITS + 1)
            nc.vector.tensor_tensor(ffn_q[:, :], ffn_q[:, :], ring[:, PRO_UNITS % 2, 0, 0:D], ALU.add).then_inc(unit_free, 1)

            def post(c, k, slot, u):
                base = DVE_POST * c
                dve.wait_ge(unit_done, u)
                if k < 2:
                    for i in range(2):
                        t = 2 * k + i
                        o = ring[:, slot, i, :].rearrange("p (h r) -> p h r", r=VW)
                        nc.vector.reciprocal(rsum[:, t, :], o[:, :, DK]).then_inc(dve_post, 1)
                        dve.wait_ge(dve_post, base + 3 * k + 2 * i + 1)
                        last = nc.vector.tensor_tensor(on[:, t, :].rearrange("p (h d) -> p h d", d=DK), o[:, :, 0:DK],
                                                       rsum[:, t, :].rearrange("p (h a) -> p h a", a=1).to_broadcast([128, H, DK]),
                                                       ALU.mult)
                        last.then_inc(*((dve_post, 1) if i == 0 else (unit_free, 1)))
                if k == 2:
                    nc.vector.tensor_copy(onT, ring[:, slot, 0, :]).then_inc(unit_free, 1)
                if k == 4:
                    nc.vector.tensor_copy(x1T, ring[:, slot, 0, :]).then_inc(unit_free, 1)
                if k in (3, 5):
                    at = base + DVE_ON + (1 if k == 3 else 1 + 2 * TPC)
                    added = x_sb[:, c * TPC:(c + 1) * TPC, :] if k == 3 else x1b[:, :, :]
                    if k == 3 and c > 0:
                        dve.wait_ge(pool_post, post_pool_count(c - 1, 1))
                    if k == 5:
                        dve.wait_ge(pool_post, post_pool_count(c, 0))
                    nc.vector.tensor_tensor(res[:, :, :], ring[:, slot, 0, :].rearrange("p (t d) -> p t d", d=D), added,
                                            ALU.add).then_inc(unit_free, 1)
                    dve.wait_ge(unit_free, 2 + u)
                    for t in range(TPC):
                        nc.vector.bn_stats(stats[:, t, :], res[:, t, :]).then_inc(dve_post, 1)
                    for t in range(TPC):
                        dve.wait_ge(dve_post, at + t)
                        nc.vector.bn_aggr(mv[:, t, :], stats[:, t, :]).then_inc(dve_post, 1)

            def body(g, last):
                u = 0
                for e in schedule(last):
                    if e[0] == "A":
                        slot = (RING_0 + u) % 2
                        u += 1
                        row_max(e[2], e[3], slot, g * GROUP_UNITS + (RING_0 + u))
                        if e[3] == score_units(e[2])[-1]:
                            combine(e[2], g * GROUP_UNITS + (RING_0 + u))
                    if e[0] == "M":
                        slot = (RING_0 + u) % 2
                        u += 1
                        rows(e[2], slot, g * GROUP_UNITS + (RING_0 + u))
                    if e[0] == "POST":
                        slot = (RING_0 + u) % 2
                        u += 1
                        post(e[1], e[2], slot, RING_0 + (NG - 1) * GROUP_UNITS + u)

            groups(dve, body)

        @block.tensor
        def _(pe):
            pe.wait_ge(consts, 6)
            pe.wait_ge(ld_w, 48)
            bank = prep_begin(pe, ("W", 0))
            for w in range(3):
                nc.tensor.transpose(bank[:, w * 128:(w + 1) * 128], wqkv_sb[:, w, :], ident[:, :])
            nc.tensor.transpose(bank[:, 384:512], wo_sb[:, :], ident[:, :]).then_inc(bank_done[0], 1)
            bank = prep_begin(pe, ("L", 0))
            nc.tensor.transpose(bank[0:RANK, 0:128], a_sb[:, :], ident[:, :]).then_inc(bank_done[1], 1)

            def prep(c):
                pe.wait_ge(ld_x[c], 16)
                bank = prep_begin(pe, ("X", c))
                for t in range(TPC):
                    last = nc.tensor.transpose(bank[:, t * TOK:(t + 1) * TOK], x_sb[:, c * TPC + t, :], ident[:, :])
                last.then_inc(bank_done[prep_bank_of(("X", c))[0]], 1)
                if c == 0:
                    pe.wait_ge(w_done, 6)
                b, n = prep_bank_of(("X", c))
                pe.wait_ge(bank_free[b], n)
                for kind, w in (("Q", wT[:, 0, :]), ("QS", wTs[:, 0, :]), ("K", wT[:, 1, :]), ("KS", wTs[:, 1, :])):
                    bank = prep_begin(pe, (kind, c))
                    nc.tensor.matmul(bank, w, xT[:, c % 2, :], start=True, stop=True).then_inc(bank_done[prep_bank_of((kind, c))[0]], 1)
                bank = prep_begin(pe, ("V", c))
                for t in range(TPC):
                    last = nc.tensor.matmul(bank[:, t * D:(t + 1) * D], xT[:, c % 2, t * TOK:(t + 1) * TOK],
                                            wT[:, 2, :], start=True, stop=True)
                last.then_inc(bank_done[prep_bank_of(("V", c))[0]], 1)

            def scores(c, unit, slot, u_free):
                kk, ii, hp = unit
                w = CH if kk < c else (ii + 1) * TOK
                pe.wait_ge(unit_free, u_free)
                for i in range(2):
                    h = 2 * hp + i
                    dst = ring[:, slot, i, :]
                    last = nc.tensor.matmul(dst[:, 0:w], qA[:, c, h, ii * TOK:(ii + 1) * TOK], kA[:, kk, h, 0:w],
                                            start=True, stop=kk < c)
                    if kk == c:
                        last = nc.tensor.matmul(dst[:, w - TOK:w], ident_h[:, :], causal[:, :], start=False, stop=True)
                last.then_inc(unit_done, 1)

            def maxima_rows(c, slot, u_free, before, n):
                pe.wait_ge(unit_free, u_free)
                pe.wait_ge(nsplit, before * 4 + 4 * n)
                nc.tensor.transpose(ring[:, slot, 0, 0:TOK // 2].bitcast(bf16), nparts[:, c, :], ident_h[:, :]).then_inc(unit_done, 1)

            for c in range(NC):
                prep(c)
            u = 0
            for c in range(2):
                pe.wait_ge(qkA_in[c], 16 * N_A)
                for unit in score_units(c):
                    scores(c, unit, u % 2, u + 1)
                    u += 1
                maxima_rows(c, u % 2, u + 1, 0, c + 1)
                u += 1
            pe.wait_ge(unit_free, u + 1)
            pe.wait_ge(ld_ffn, 48)
            pe.wait_ge(bank_free[1], 1)
            nc.tensor.matmul(ring[:, u % 2, 0, 0:D], aT[:, :], b_sb[:, :], start=True, stop=True).then_inc(unit_done, 1)
            pe.sem_inc(probs_free, PRING)
            for b in range(4):
                pe.wait_ge(bank_free[b], (len(PREP) - b + 3) // 4)

            def post(c, k, slot, u_free):
                base = DVE_POST * c
                pe.wait_ge(unit_free, u_free)
                if k < 2:
                    pe.wait_ge(o_free, 2 + (NG - 1) * NC + c + 1)
                    for i in range(2):
                        t = c * TPC + 2 * k + i
                        for g in range(NG):
                            last = nc.tensor.transpose(ring[:, slot, i, g * 128:(g + 1) * 128],
                                                       oT[:, g, t * TOK:(t + 1) * TOK], ident[:, :])
                if k == 2:
                    pe.wait_ge(unit_free, u_free + 1)
                    for t in range(TPC):
                        last = nc.tensor.transpose(ring[:, slot, 0, t * TOK:(t + 1) * TOK], on[:, t, :], ident[:, :])
                if k == 3:
                    pe.wait_ge(unit_free, u_free + 1)
                    for t in range(TPC):
                        last = nc.tensor.matmul(ring[:, slot, 0, t * D:(t + 1) * D], onT[:, t * TOK:(t + 1) * TOK],
                                                wT[:, 3, :], start=True, stop=True)
                if k == 4:
                    pe.wait_ge(pool_post, post_pool_count(c, 0) - TPC)
                    for t in range(TPC):
                        last = nc.tensor.transpose(ring[:, slot, 0, t * TOK:(t + 1) * TOK], x1[:, t, :], ident[:, :])
                if k == 5:
                    pe.wait_ge(unit_free, u_free + 1)
                    for t in range(TPC):
                        last = nc.tensor.matmul(ring[:, slot, 0, t * D:(t + 1) * D], x1T[:, t * TOK:(t + 1) * TOK],
                                                ffn_q[:, :], start=True, stop=True)
                last.then_inc(unit_done, 1)

            def body(g, last):
                u, split = 0, 2
                for e in schedule(last):
                    if e[0] in RING_EVENTS:
                        slot = (RING_0 + u) % 2
                        u_free = g * GROUP_UNITS + (RING_0 + u + 1)
                        u += 1
                    if e[0] == "A":
                        if e[3] == (0, 0, 0):
                            for k in (range(e[2] + 1) if not e[1] else [e[2]]):
                                pe.wait_ge(qkA_in[k], g * 16 * N_A + (1 + e[1]) * 16 * N_A)
                        scores(e[2], e[3], slot, u_free)
                    if e[0] == "M":
                        split += 1
                        maxima_rows(e[2], slot, u_free, g * 4, split)
                    if e[0] == "S":
                        c, j = e[1], e[2]
                        J = step_index(c, j)
                        lo = max(0, j - TPC * c) * TOK
                        if j == 0 and e[3] == 0:
                            pe.wait_ge(qkB_in[c], g * 32 + 32)
                            pe.wait_ge(mrow_in[c], g * 48 + 48)
                        for h in (2 * e[3], 2 * e[3] + 1):
                            pe.wait_ge(exp_done, g * BLOCKS + (J * HG + h + 1))
                            nc.tensor.matmul(sT[:, h % 2, lo:CH], kB[:, j // TPC, h, (j % TPC) * TOK:(j % TPC + 1) * TOK],
                                             qB[:, c, h, lo:CH], start=True, stop=True).then_inc(s_done, 1)
                    if e[0] == "PV":
                        c, j = e[1], e[2]
                        J = step_index(c, j)
                        lo = max(0, j - TPC * c) * TOK
                        if j == 0:
                            pe.wait_ge(o_free, g * NC + (c + 1))
                            pe.wait_ge(v_staged, g * NC + (4 + c + 1))
                        if j >= TPC * c:
                            pe.wait_ge(masked, g * (NC * TPC) + (j + 1))
                        else:
                            pe.wait_ge(exp_done, g * BLOCKS + (2 + (J + 1) * HG))
                        for h in range(HG):
                            last_pv = nc.tensor.matmul(oP[VW * h:VW * (h + 1), c % 2, lo:CH], v_g[:, j, h, :],
                                                       probs[:, J % PRING, h, lo:CH], start=j == 0,
                                                       stop=j == TPC * (c + 1) - 1)
                        last_pv.then_inc(probs_free, 1)
                    if e[0] == "POST":
                        post(e[1], e[2], slot, u_free)

            groups(pe, body)


_INS = ['L0_attn_x', 'L0_attn_W_qkv', 'L0_attn_W_o', 'L0_ffn_kernel', 'L0_ffn_bias', 'L0_ffn_a', 'L0_ffn_b']
_OUTS = [((1, S, D), 'float32')]


def kernel(**inputs):
    import numpy as _np
    import concourse.bacc as _bacc
    from concourse import mybir as _mybir
    from concourse.bass_utils import run_bass_kernel_spmd as _run

    nc = _bacc.Bacc("TRN2", target_bir_lowering=False, num_devices=1)
    arrays, args = {}, []
    for name in _INS:
        a = _np.ascontiguousarray(inputs[name])
        arrays[f"in_{name}_dram"] = a
        args.append(nc.dram_tensor(f"in_{name}_dram", a.shape, _mybir.dt.from_np(a.dtype), kind="ExternalInput").ap())
    tables = rope_tables()
    arrays["rope_tables_dram"] = tables
    args.append(nc.dram_tensor("rope_tables_dram", tables.shape, _mybir.dt.from_np(tables.dtype), kind="ExternalInput").ap())
    for i, (shape, dtype) in enumerate(_OUTS):
        dt = _mybir.dt.from_np(_np.dtype(dtype))
        args.append(nc.dram_tensor(f"out_{i}_dram", shape, dt, kind="ExternalOutput").ap())
    attention_block(nc, *args)
    r = _run(nc, [arrays], core_ids=[0])
    got = tuple(r.results[0][f"out_{i}_dram"] for i in range(len(_OUTS)))
    return got[0]
```

```python
import numpy as np
import concourse.bass as bass
from concourse import mybir
from contextlib import ExitStack

S, D, H, DK = 2048, 128, 16, 8
RANK = 16
THETA = 10000.0
TOK = 128
CH = 512
NT, NC, TPC = S // TOK, S // CH, CH // TOK
HG = 4
NG = H // HG
PARTS = 3
TERMS = PARTS * PARTS * DK
SHIFT_ROW = 96
KROWS = 128
VW = 32
SBANKS = 3
PRING = 4
NEG = -3.0e38
EPS = 1e-5
ONE_PAIR = 1.0 + 0x3F80 / 2 ** 23


def rope_tables():
    inv = np.float32(THETA) ** (-np.arange(0, DK, 2, dtype=np.float32) / np.float32(DK))
    ang = np.arange(S, dtype=np.float32)[None, :] * inv.astype(np.float32)[:, None]
    cos = np.repeat(np.cos(ang), 2, axis=0)
    sin = np.repeat(np.sin(ang), 2, axis=0)
    sin[0::2] *= -1
    rows = [np.tile(np.repeat(t, HG, axis=0), (NG, 1)) for t in (cos, sin)]
    return np.ascontiguousarray(np.stack(rows).astype(np.float32))


def score_units(c):
    return [(kk, ii, hp) for kk in range(c + 1) for ii in range(TPC) for hp in range(HG // 2)]


def pace(work, weights, cost):
    total, whole = sum(cost(w) for w in work), sum(weights)
    out, spent, at, passed = [], 0.0, 0, 0.0
    for w in weights:
        passed += w
        here = []
        while at < len(work) and spent + 0.5 * cost(work[at]) <= total * passed / whole + 1e-6:
            here.append(work[at])
            spent += cost(work[at])
            at += 1
        out.append(here)
    out[-1] += work[at:]
    return out


def reduce_cost(e):
    if e[0] != "A":
        return 0.0
    kk, ii, _ = e[3]
    return 64 + 2 * (CH if kk < e[2] else (ii + 1) * TOK)


def maxima_order(nxt, c, units, after):
    return ([("A", nxt, c, u) for u in units] + after[:2] + [("N", nxt, c)] + after[2:6] + [("M", nxt, c)] + after[6:])


AHEAD = TPC * (HG // 2)


def early_units(nxt):
    two = [("A", nxt, 2, u) for u in score_units(2)[:AHEAD]]
    return maxima_order(nxt, 0, score_units(0), maxima_order(nxt, 1, score_units(1), two))


def prologue():
    e = early_units(0)
    return [("P", 0), ("P", 1), ("P", 2)] + e[:8] + [("P", 3)] + e[8:]


def schedule(last):
    steps = [(c, j) for c in range(NC) for j in range(TPC * (c + 1))]
    weight = {(c, j): min(1.0, (TPC * (c + 1) - j) / TPC) for c, j in steps}
    post = {}
    if last:
        for c in range(NC - 1):
            for e, at in zip(POST_ORDER, POST_STEPS[c]):
                post.setdefault(steps[step_index(c + 1, 0) + at], []).append((e[0], c, e[1]))
    main, pv = [], []
    for c, j in steps:
        main.append(([("S", c, j, 0)], FILL[0] * weight[c, j]))
        if len(pv) > 1:
            main.append(([("PV",) + pv[0]], FILL[1] * weight[pv.pop(0)]))
        main.append(([("S", c, j, 1)] + post.get((c, j), []), FILL[2] * weight[c, j]))
        pv.append((c, j))
    main += [([("PV",) + p], FILL[1] * weight[p]) for p in pv]
    third = [("A", 0, 3, u) for u in score_units(3)]
    here = maxima_order(0, 2, score_units(2)[AHEAD:], third[:])
    filler = maxima_order(0, 3, [], early_units(1) if not last else [])
    due = next(i for i, (es, _) in enumerate(main) if es[0] == ("S", NC - 1, 0, 0)) - DUE
    n_due = filler.index(("M", 0, 3)) + 1
    fill = pace(here + filler[:n_due], [w for _, w in main[:due]], reduce_cost)
    fill += pace(filler[n_due:], [w for _, w in main[due:]], reduce_cost)
    out = []
    for (es, _), work in zip(main, fill):
        out += es + work
    if last:
        out += [(e[0], NC - 1, e[1]) for e in POST_ORDER]
    return out


POST_ORDER = (("POST", 0), ("POST", 1), ("POST", 2), ("POST", 3), ("NORM", 0), ("POST", 4), ("POST", 5), ("NORM", 1))
POST_STEPS = [(3, 3, 4, 5, 6, 6, 7, 8), (3, 4, 5, 6, 7, 7, 8, 9), (3, 4, 5, 6, 7, 7, 8, 9)]


def step_index(c, j):
    return sum(TPC * (b + 1) for b in range(c)) + j


FILL = (0, 1, 2)
DUE = 5
RING_EVENTS = ("A", "M", "POST")
PRO_UNITS = sum(e[0] in RING_EVENTS for e in early_units(0))
RING_0 = PRO_UNITS + 1
GROUP_UNITS = sum(e[0] in RING_EVENTS for e in schedule(False))
STEPS = sum(TPC * (c + 1) for c in range(NC))
BLOCKS = STEPS * HG


def attention_block(nc, x, w_qkv, w_o, ffn_w, ffn_bias, lora_a, lora_b, tables, out):
    fp32, bf16 = mybir.dt.float32, mybir.dt.bfloat16
    ALU, ACT, AX = mybir.AluOpType, mybir.ActivationFunctionType, mybir.AxisListType
    absmax = bass.bass_isa.ReduceOp.absmax

    x_t = x.rearrange("a (t p) d -> p (a t) d", p=TOK)
    out_t = out.rearrange("a (t p) d -> p (a t) d", p=TOK)

    ctx = ExitStack()
    with ctx:
        def sb(name, shape, dt=fp32):
            return ctx.enter_context(nc.sbuf_tensor(name, shape, dt))

        def sem(name):
            return ctx.enter_context(nc.semaphore(name))

        x_sb = sb("x_sb", [128, NT, D])
        wqkv_sb = sb("wqkv_sb", [128, 3, D])
        wo_sb = sb("wo_sb", [128, D])
        ffn_sb = sb("ffn_sb", [128, D])
        a_sb = sb("a_sb", [128, RANK])
        b_sb = sb("b_sb", [RANK, D])
        bias_sb = sb("bias_sb", [128, D])
        ident = sb("ident", [128, 128])
        ident_h = sb("ident_h", [128, 128], bf16)
        causal = sb("causal", [128, 128], bf16)
        wT = sb("wT", [128, 4, D])
        wTs = sb("wTs", [128, 2, D])
        aT = sb("aT", [RANK, 128])
        ffn_q = sb("ffn_q", [128, D])
        wst = sb("wst", [128, 8])
        rot = sb("rot", [128, 2, 3, CH])
        qp = sb("qp", [128, 2, PARTS, CH], bf16)
        kp = sb("kp", [128, 2, PARTS, CH], bf16)
        q_dram = nc.dram_tensor("q_parts", [NC, PARTS, NG, DK * HG, CH], bf16, kind="Internal").ap()
        k_dram = nc.dram_tensor("k_parts", [NC, PARTS, NG, DK * HG, CH], bf16, kind="Internal").ap()
        v_all = sb("v_all", [128, NT, H, DK])
        qA = sb("qA", [128, NC, HG, CH], bf16)
        kA = sb("kA", [128, NC, HG, CH], bf16)
        qB = sb("qB", [128, NC, HG, CH], bf16)
        kB = sb("kB", [128, NC, HG, CH], bf16)
        v_g = sb("v_g", [128, NT, HG, VW])
        pmax = sb("pmax", [128, NC, HG, TPC, NC])
        nmax = sb("nmax", [128, NC, HG * TPC])
        nrest = sb("nrest", [128, NC, HG * TPC])
        nparts = sb("nparts", [128, NC, 128], bf16)
        mrows = sb("mrows", [PARTS * HG * TPC, NC, TOK], bf16)
        probs = sb("probs", [128, PRING, HG, CH])
        xT = probs[:, 0, 0:2, :]
        cs_sb = [probs[:, 1 + c // 2, 2 * (c % 2):2 * (c % 2) + 2, :] for c in range(NC)]
        oT = sb("oT", [128, NG, S])
        rsum = sb("rsum", [128, TPC, H])
        on, res, x1 = (rot[:, 0, i, :].rearrange("p (t d) -> p t d", d=D) for i in range(3))
        onT, x1T = rot[:, 1, 0, :], rot[:, 1, 1, :]
        x1b = rot[:, 1, 2, :].rearrange("p (t d) -> p t d", d=D)
        stats = sb("stats", [128, TPC, 6])
        mv = sb("mv", [128, TPC, 2])
        rstd = sb("rstd", [128, TPC])
        mhalf = sb("mhalf", [128, TPC])
        y_sb = sb("y_sb", [128, TPC, D])

        ring = ctx.enter_context(nc.psum_tensor("ring", [128, 2, 2, CH], fp32))
        sT = ctx.enter_context(nc.psum_tensor("sT", [128, SBANKS, CH], fp32))
        oP = ctx.enter_context(nc.psum_tensor("oP", [128, CH], fp32))
        prep_bank = [sT[:, 0, :], sT[:, 1, :], sT[:, 2, :], oP[:, :]]

        ld_w = sem("ld_w")
        ld_ffn = sem("ld_ffn")
        ld_x = [sem(f"ld_x{c}") for c in range(NC)]
        ld_cs = [sem(f"ld_cs{c}") for c in range(NC)]
        consts = sem("consts")
        filled = sem("filled")
        filled_b = sem("filled_b")
        bank_done = [sem(f"bank_done{b}") for b in range(4)]
        bank_free = [sem(f"bank_free{b}") for b in range(4)]
        rope_sum, part_done, rest_done = ([sem(f"{n}_{w}") for w in "qk"] for n in ("rope_sum", "part_done", "rest_done"))
        w_done = sem("w_done")
        wq_step = sem("wq_step")
        parts_out = [[sem(f"{w}parts_out{c}") for w in "qk"] for c in range(NC)]
        qkA_in = [sem(f"qkA_in{c}") for c in range(NC)]
        qkB_in = [sem(f"qkB_in{c}") for c in range(NC)]
        unit_done = sem("unit_done")
        unit_free = sem("unit_free")
        nmax_done = sem("nmax_done")
        nsplit = sem("nsplit")
        mrow_in = [sem(f"mrow_in{c}") for c in range(NC)]
        s_done = sem("s_done")
        exp_done = sem("exp_done")
        masked = sem("masked")
        gate = sem("gate")
        probs_free = sem("probs_free")
        o_free = sem("o_free")
        v_staged = sem("v_staged")
        dve_post = sem("dve_post")
        pool_post = sem("pool_post")
        normed = sem("normed")
        stored = sem("stored")

        block = ctx.enter_context(nc.Block())

        def groups(eng, body):
            with eng.Fori(0, NG - 1) as g:
                body(g, False)
            body(NG - 1, True)

        PREP = [("W", 0), ("L", 0)]
        PREP += [("X", 0)]
        for c in range(NC):
            PREP += [(k, c) for k in ("Q", "QS", "K", "KS")] + ([("X", c + 1)] if c < NC - 1 else []) + [("V", c)]
        PREP_AT = {u: n for n, u in enumerate(PREP)}

        def prep_bank_of(u):
            return PREP_AT[u] % 4, PREP_AT[u] // 4 + 1

        def prep_begin(pe, u):
            b, n = prep_bank_of(u)
            if n > 1:
                pe.wait_ge(bank_free[b], n - 1)
            return prep_bank[b]

        def prep_read(eng, u):
            b, n = prep_bank_of(u)
            eng.wait_ge(bank_done[b], n)
            return prep_bank[b]

        def store_parts(sp, c):
            for w, (parts, dram) in enumerate(((qp, q_dram), (kp, k_dram))):
                sp.wait_ge(part_done[w], 2 * (c + 1))
                sp.wait_ge(rest_done[w], 2 * (c + 1))
                sp.dma_start(dram[c, :, :, :, :].rearrange("a g r s -> (g r) a s"), parts[:, c % 2, :, :]).then_inc(parts_out[c][w], 16)

        N_A = 2 * PARTS

        def load_A(sp, c, g, first=False):
            for w, (operand, dram) in enumerate(((qA, q_dram), (kA, k_dram))):
                if first:
                    sp.wait_ge(parts_out[c][w], 16)
                for a in range(PARTS):
                    rows = operand[a * PARTS * DK:(a + 1) * PARTS * DK, c, :, :].rearrange("r h s -> r (h s)")
                    if w == 0:
                        part = dram[c, a, bass.ds(g, 1), :, :].rearrange("x (d h) s -> x d (h s)", h=HG)\
                            .to_broadcast([PARTS, DK, HG * CH])
                    else:
                        part = dram[c, :, bass.ds(g, 1), :, :].rearrange("b x (d h) s -> b (x d) (h s)", h=HG)
                    sp.dma_start(rows, part).then_inc(qkA_in[c], 16)

        def load_B(sp, c):
            sp.dma_start(qB[0:TERMS, c, :, :], qA[0:TERMS, c, :, :]).then_inc(qkB_in[c], 16)
            sp.dma_start(kB[0:TERMS, c, :, :], kA[0:TERMS, c, :, :]).then_inc(qkB_in[c], 16)

        def load_maxima(sp, c, u_free):
            sp.wait_ge(unit_free, u_free)
            sp.dma_start(qB[SHIFT_ROW:SHIFT_ROW + PARTS, c, :, :], mrows[:, c, :]).then_inc(mrow_in[c], 16)

        POOL_1, POOL_2 = 3, 2

        def pool_count(c, norm):
            return c * (POOL_1 + POOL_2) + (POOL_1 + POOL_2 if norm else 2)

        def normed_count(c, norm):
            return (2 * c + norm + 1) * TPC

        DVE_ON = 2
        DVE_POST = DVE_ON + 2 * (2 * TPC)

        @block.sync
        def _(sp):
            sp.dma_start(x_sb[:, 0:TPC, :], x_t[:, 0:TPC, :]).then_inc(ld_x[0], 16)
            sp.dma_start(wqkv_sb[:, :, :], w_qkv.rearrange("(k p) d -> p k d", p=128)).then_inc(ld_w, 16)
            sp.dma_start(wo_sb[:, :], w_o).then_inc(ld_w, 16)
            sp.dma_start(a_sb[:, :], lora_a).then_inc(ld_w, 16)
            for c in range(NC):
                sp.dma_start(cs_sb[c],
                             tables[:, :, c * CH:(c + 1) * CH].rearrange("w p s -> p w s")).then_inc(ld_cs[c], 16)
            for c in range(1, NC):
                sp.dma_start(x_sb[:, c * TPC:(c + 1) * TPC, :], x_t[:, c * TPC:(c + 1) * TPC, :]).then_inc(ld_x[c], 16)
            sp.dma_start(ffn_sb[:, :], ffn_w).then_inc(ld_ffn, 16)
            sp.dma_start(b_sb[:, :], lora_b).then_inc(ld_ffn, 16)
            sp.dma_start(bias_sb[:, :], ffn_bias.rearrange("(a n) -> a n", a=1).to_broadcast([128, D])).then_inc(ld_ffn, 16)
            sp.wait_ge(filled, 2)
            u = 0
            for e in prologue():
                u += e[0] in RING_EVENTS
                if e[0] == "P":
                    c = e[1]
                    store_parts(sp, c)
                    load_A(sp, c, 0, True)
                    if c == 1:
                        sp.wait_ge(filled_b, 4)
                    for b in ([c - 1] if c == 1 or c == 2 else [c - 1, c] if c == 3 else []):
                        sp.wait_ge(qkA_in[b], 16 * N_A)
                        load_B(sp, b)
                if e[0] == "M":
                    load_maxima(sp, e[2], 2 + u)

            def body(g, last):
                u = 0
                for e in schedule(last):
                    u += e[0] in RING_EVENTS
                    if e[0] == "M":
                        load_maxima(sp, e[2], g * GROUP_UNITS + (2 + RING_0 + u))
                    free = None
                    if e[0] == "A" and e[2] == 3 and e[3][1:] == (TPC - 1, HG // 2 - 1) and e[3][0] < NC - 1:
                        free = e[3][0]
                    if e[0] == "M" and e[2] == NC - 1:
                        free = NC - 1
                    if free is not None and not last:
                        sp.wait_ge(unit_done, g * GROUP_UNITS + (RING_0 + u))
                        sp.wait_ge(qkB_in[free], g * 32 + 32)
                        load_A(sp, free, g + 1)
                    if e[0] == "S" and not last and e[1] == NC - 1 and e[3] == 1 and e[2] % TPC == TPC - 1:
                        c = e[2] // TPC
                        sp.wait_ge(s_done, g * BLOCKS + (step_index(NC - 1, e[2]) + 1) * HG)
                        sp.wait_ge(qkA_in[c], g * 16 * N_A + 2 * 16 * N_A)
                        load_B(sp, c)
                    if e[0] == "NORM" and e[2] == 1:
                        c = e[1]
                        sp.wait_ge(normed, normed_count(c, 1))
                        sp.dma_start(out_t[:, c * TPC:(c + 1) * TPC, :], y_sb[:, :, :]).then_inc(stored, 16)

            groups(sp, body)
            sp.wait_ge(stored, 16 * NC)

        def stage_v(pool, c, g):
            tiles = slice(c * TPC, (c + 1) * TPC)
            nc.gpsimd.tensor_copy(v_g[:, tiles, :, 0:DK], v_all[:, tiles, bass.ds(g * HG, HG), :]).then_inc(v_staged, 1)

        def add_rotation(eng, ops, c, w):
            for kind in (("Q", "QS"), ("K", "KS"))[w]:
                b, uses = prep_bank_of((kind, c))
                eng.wait_ge(bank_free[b], uses)
            if c > 0:
                eng.wait_ge(rest_done[w], 2 * c)
            ops.tensor_tensor(rot[:, w, 2, :], rot[:, w, 0, :], rot[:, w, 1, :], ALU.add).then_inc(rope_sum[w], 1)

        def split_rotation(eng, ops, c, w, parts):
            eng.wait_ge(rope_sum[w], c + 1)
            eng.wait_ge(part_done[w], 2 * c + 1)
            ops.tensor_tensor(rot[:, w, 2, :], rot[:, w, 2, :], parts[:, c % 2, 0, :], ALU.subtract).then_inc(rest_done[w], 1)
            eng.wait_ge(rest_done[w], 2 * c + 1)
            eng.wait_ge(part_done[w], 2 * c + 2)
            ops.tensor_tensor(parts[:, c % 2, 2, :], rot[:, w, 2, :], parts[:, c % 2, 1, :], ALU.subtract).then_inc(rest_done[w], 1)

        def stage_v_in(pool, c):
            b, uses = prep_bank_of(("V", c))
            pool.wait_ge(bank_free[b], uses)
            pool.wait_ge(v_staged, 4)
            stage_v(pool, c, 0)

        def split_maxima(pool, c, before, n):
            n_m = HG * TPC
            part = [nparts[:, c, a * n_m:(a + 1) * n_m] for a in range(PARTS)]
            pool.wait_ge(nmax_done, before + n)
            pool.sem_inc(gate, 1)
            nc.gpsimd.tensor_copy(part[0], nmax[:, c, :]).then_inc(nsplit, 1)
            pool.wait_ge(nsplit, before * 4 + (4 * n - 3))
            nc.gpsimd.tensor_tensor(nrest[:, c, :], nmax[:, c, :], part[0], ALU.subtract).then_inc(nsplit, 1)
            pool.wait_ge(nsplit, before * 4 + (4 * n - 2))
            pool.sem_inc(gate, 1)
            nc.gpsimd.tensor_copy(part[1], nrest[:, c, :]).then_inc(nsplit, 1)
            pool.wait_ge(nsplit, before * 4 + (4 * n - 1))
            nc.gpsimd.tensor_tensor(part[2], nrest[:, c, :], part[1], ALU.subtract).then_inc(nsplit, 1)

        def post_rstd(pool, c, norm):
            base = pool_count(c, norm) - 2
            pool.wait_ge(dve_post, DVE_POST * c + DVE_ON + (norm + 1) * 2 * TPC)
            nc.gpsimd.tensor_scalar(rstd[:, :], mv[:, :, 1], EPS, None, ALU.add).then_inc(pool_post, 1)
            pool.wait_ge(pool_post, base + 1)
            nc.gpsimd.tensor_tensor(rstd[:, :], rstd[:, :], mhalf[:, :], ALU.pow).then_inc(pool_post, 1)

        def post_bias(pool, c):
            pool.wait_ge(normed, normed_count(c, 0))
            nc.gpsimd.tensor_tensor(x1b[:, :, :], x1[:, :, :],
                                    bias_sb[:, :].rearrange("p (a d) -> p a d", a=1).to_broadcast([128, TPC, D]),
                                    ALU.add).then_inc(pool_post, 1)

        @block.gpsimd
        def _(pool):
            pool.memset(ident[:, :], 0.0).then_inc(consts, 1)
            pool.memset(ident_h[:, :], 0.0).then_inc(consts, 1)
            pool.memset(causal[:, :], 0.0).then_inc(consts, 1)
            pool.wait_ge(consts, 3)
            for m in (ident, ident_h):
                pool.affine_select(out=m[:, :], in_=m[:, :], compare_op=ALU.not_equal, fill=1.0, base=0,
                                   pattern=[[-1, 128]], channel_multiplier=1).then_inc(consts, 1)
            pool.affine_select(out=causal[:, :], in_=causal[:, :], compare_op=ALU.is_ge, fill=NEG, base=0,
                               pattern=[[-1, 128]], channel_multiplier=1).then_inc(consts, 1)
            pool.memset(v_g[:, :, :, :], 0.0).then_inc(v_staged, 1)
            pool.wait_ge(v_staged, 1)
            pool.memset(v_g[:, :, :, DK:DK + 1], 1.0).then_inc(v_staged, 1)
            pool.memset(mhalf[:, :], -0.5).then_inc(v_staged, 1)
            pool.memset(nparts[:, :, :], 0.0).then_inc(v_staged, 1)
            pool.wait_ge(v_staged, 4)
            pool.memset(kB[64:96, :, :, :].bitcast(fp32), 0.0).then_inc(filled_b, 1)
            pool.wait_ge(filled_b, 1)
            pool.memset(kB[96:128, :, :, :].bitcast(fp32), ONE_PAIR).then_inc(filled_b, 1)
            pool.wait_ge(filled_b, 2)
            split = 0
            for e in prologue():
                if e[0] == "P":
                    add_rotation(pool, nc.gpsimd, e[1], 1)
                    split_rotation(pool, nc.gpsimd, e[1], 1, kp)
                    stage_v_in(pool, e[1])
                if e[0] == "P" and e[1] < 2:
                    pool.wait_ge(v_staged, 4 + e[1] + 1)
                    pool.memset(qB[64:128, 2 * e[1]:2 * e[1] + 2, :, :].bitcast(fp32), 0.0).then_inc(filled_b, 1)
                    pool.wait_ge(filled_b, 3 + e[1])
                if e[0] == "N":
                    split += 1
                    split_maxima(pool, e[2], 0, split)
            pool.wait_ge(ld_ffn, 48)
            pool.wait_ge(wq_step, 1)
            nc.gpsimd.partition_all_reduce(wst[:, 1:2], wst[:, 0:1], 128, absmax).then_inc(wq_step, 1)
            for n, (o, a, k, b, op) in enumerate(((2, 1, 1.0 / 7.0, None, None), (4, 2, 8.0, 1, ALU.subtract), (4, 2, 1.0, 4, ALU.subtract),
                                                  (4, 4, 1.0 / 7.0, 2, ALU.add))):
                pool.wait_ge(wq_step, n + 2)
                if b is None:
                    nc.gpsimd.tensor_scalar(wst[:, o:o + 1], wst[:, a:a + 1], k, None, ALU.mult).then_inc(wq_step, 1)
                else:
                    nc.gpsimd.tensor_scalar(wst[:, o:o + 1], wst[:, a:a + 1], k, wst[:, b:b + 1], ALU.mult, op).then_inc(wq_step, 1)

            def body(g, last):
                n_split = 2
                for e in schedule(last):
                    if e[0] == "S" and e[3] == 1 and e[2] >= TPC * e[1]:
                        c, jj = e[1], e[2] - TPC * e[1]
                        J = step_index(c, e[2])
                        pool.wait_ge(exp_done, g * BLOCKS + (SBANKS + (J + 1) * HG))
                        pool.sem_inc(gate, 1)
                        p = probs[:, J % PRING, :, jj * TOK:(jj + 1) * TOK]
                        pool.affine_select(out=p, in_=p, compare_op=ALU.is_ge, fill=0.0, base=0,
                                           pattern=[[0, HG], [1, TOK]], channel_multiplier=-1).then_inc(masked, 1)
                    if e[0] == "N":
                        n_split = n_split + 1
                        split_maxima(pool, e[2], g * 4, n_split)
                    if e[0] == "PV" and not last and e[1] == NC - 1 and e[2] % TPC == TPC - 1:
                        c = e[2] // TPC
                        pool.wait_ge(probs_free, g * STEPS + (PRING + step_index(NC - 1, e[2]) + 1))
                        pool.sem_inc(gate, 1)
                        stage_v(pool, c, g + 1)
                    if e[0] == "POST" and e[2] in (3, 5):
                        post_rstd(pool, e[1], 0 if e[2] == 3 else 1)
                    if e[0] == "NORM" and e[2] == 0:
                        post_bias(pool, e[1])

            groups(pool, body)

        @block.scalar
        def _(act):
            def evac(u, dst, src_of, done=None):
                src = prep_read(act, u)
                ins = nc.scalar.copy(dst, src_of(src))
                ins.then_inc(bank_free[prep_bank_of(u)[0]], 1)

            src = prep_read(act, ("W", 0))
            for w in range(2):
                nc.scalar.copy(wT[:, w, :].rearrange("p (g d h) -> p g h d", g=NG, d=DK),
                               src[:, w * D:(w + 1) * D].rearrange("p (g h d) -> p g h d", g=NG, d=DK)).then_inc(w_done, 1)
            nc.scalar.copy(wT[:, 2:4, :], src[:, 2 * D:4 * D].rearrange("p (w d) -> p w d", w=2)).then_inc(bank_free[0], 1)
            act.wait_ge(w_done, 2)
            for w in range(2):
                src = wT[:, w, :].rearrange("p (n e h) -> p n e h", e=2, h=HG)
                dst = wTs[:, w, :].rearrange("p (n e h) -> p n e h", e=2, h=HG)
                for e in range(2):
                    nc.scalar.copy(dst[:, :, e, :], src[:, :, 1 - e, :]).then_inc(w_done, 1)
            evac(("L", 0), aT[:, :], lambda s: s[0:RANK, 0:128])
            evac(("X", 0), xT[:, 0, :], lambda s: s)
            for c in range(NC):
                for w, parts in ((0, qp), (1, kp)):
                    if c >= 2:
                        act.wait_ge(parts_out[c - 2][w], 16)
                    act.wait_ge(rope_sum[w], c + 1)
                    nc.scalar.copy(parts[:, c % 2, 0, :], rot[:, w, 2, :]).then_inc(part_done[w], 1)
                    if w == 0 and c + 1 < NC:
                        if c > 0:
                            b, n = prep_bank_of(("V", c - 1))
                            act.wait_ge(bank_done[b], n)
                        evac(("X", c + 1), xT[:, (c + 1) % 2, :], lambda s: s)
                    act.wait_ge(rest_done[w], 2 * c + 1)
                    nc.scalar.copy(parts[:, c % 2, 1, :], rot[:, w, 2, :]).then_inc(part_done[w], 1)
                src = prep_read(act, ("V", c))
                b = prep_bank_of(("V", c))[0]
                nc.scalar.copy(v_all[:, c * TPC:(c + 1) * TPC, :, :],
                               src.rearrange("p (t h d) -> p t h d", t=TPC, h=H)).then_inc(bank_free[b], 1)
            act.sem_inc(exp_done, SBANKS)
            act.sem_inc(o_free, 1)

            def flush_o(g, c):
                act.wait_ge(probs_free, g * STEPS + (PRING + step_index(c, TPC * (c + 1) - 1) + 1))
                nc.scalar.copy(oT[:, bass.ds(g, 1), c * CH:(c + 1) * CH],
                               oP[:, :].rearrange("p (a s) -> p a s", a=1)).then_inc(o_free, 1)

            def body(g, last):
                for e in schedule(last):
                    if e[0] == "S":
                        c, j = e[1], e[2]
                        J = step_index(c, j)
                        lo = max(0, j - TPC * c) * TOK
                        act.wait_ge(probs_free, g * STEPS + (J + 1))
                        for h in (2 * e[3], 2 * e[3] + 1):
                            act.wait_ge(s_done, g * BLOCKS + (J * HG + h + 1))
                            nc.scalar.activation(probs[:, J % PRING, h, lo:CH], sT[:, (J * HG + h) % SBANKS, lo:CH], ACT.Exp,
                                                 scale=float(DK) ** -0.5).then_inc(exp_done, 1)
                    if e[0] == "PV" and e[2] == TPC * (e[1] + 1) - 1:
                        flush_o(g, e[1])

            groups(act, body)

        @block.vector
        def _(dve):
            nc.vector.memset(qA[64:128, :, :, :].bitcast(fp32), 0.0).then_inc(filled, 1)
            nc.vector.memset(kA[64:128, :, :, :].bitcast(fp32), 0.0).then_inc(filled, 1)
            dve.sem_inc(unit_free, 2)

            def rotate(c):
                dve.wait_ge(ld_cs[c], 16)
                for w, names in ((0, ("Q", "QS")), (1, ("K", "KS"))):
                    if c > 0:
                        dve.wait_ge(rope_sum[w], c)
                    for i, kind in enumerate(names):
                        src = prep_read(dve, (kind, c))
                        b = prep_bank_of((kind, c))[0]
                        nc.vector.tensor_tensor(rot[:, w, i, :], src, cs_sb[c][:, i, :], ALU.mult).then_inc(bank_free[b], 1)
                    if w == 0:
                        add_rotation(dve, nc.vector, c, 0)
                split_rotation(dve, nc.vector, c, 0, qp)

            def row_max(c, unit, slot, u):
                kk, ii, hp = unit
                w = CH if kk < c else (ii + 1) * TOK
                dve.wait_ge(unit_done, u)
                nc.vector.tensor_reduce(pmax[:, c, 2 * hp:2 * hp + 2, ii, kk], ring[:, slot, :, 0:w],
                                        AX.X, ALU.max).then_inc(unit_free, 1)

            def combine(c, u):
                dve.wait_ge(unit_free, 2 + u)
                nc.vector.tensor_reduce(nmax[:, c, :], pmax[:, c, :, :, 0:c + 1].rearrange("p h i k -> p (h i) k"),
                                        AX.X, ALU.max, negate=True).then_inc(nmax_done, 1)

            def rows(c, slot, u):
                dve.wait_ge(unit_done, u)
                nc.vector.tensor_copy(mrows[:, c, :], ring[0:PARTS * HG * TPC, slot, 0, 0:TOK // 2].bitcast(bf16)).then_inc(unit_free, 1)

            u = 0
            for e in prologue():
                if e[0] == "P":
                    rotate(e[1])
                if e == ("P", 1):
                    dve.wait_ge(ld_ffn, 48)
                    nc.vector.tensor_reduce(wst[:, 0:1], ffn_sb[:, :], AX.X, ALU.max, apply_absolute_value=True).then_inc(wq_step, 1)
                if e[0] == "A":
                    row_max(e[2], e[3], u % 2, u + 1)
                    u += 1
                    if e[3] == score_units(e[2])[-1]:
                        combine(e[2], u)
                if e[0] == "M":
                    rows(e[2], u % 2, u + 1)
                    u += 1
            dve.wait_ge(wq_step, 6)
            nc.vector.reciprocal(wst[:, 3:4], wst[:, 4:5]).then_inc(wq_step, 1)
            dve.wait_ge(wq_step, 7)
            nc.vector.tensor_scalar(ffn_q[:, :], ffn_sb[:, :], wst[:, 3:4], None, ALU.mult).then_inc(wq_step, 1)
            dve.wait_ge(wq_step, 8)
            nc.vector.tensor_scalar(ffn_q[:, :], ffn_q[:, :], 12582912.0, 12582912.0, ALU.add, ALU.subtract).then_inc(wq_step, 1)
            dve.wait_ge(wq_step, 9)
            nc.vector.tensor_scalar(ffn_q[:, :], ffn_q[:, :], -8.0, 7.0, ALU.max, ALU.min).then_inc(wq_step, 1)
            dve.wait_ge(wq_step, 10)
            nc.vector.tensor_scalar(ffn_q[:, :], ffn_q[:, :], wst[:, 4:5], None, ALU.mult).then_inc(wq_step, 1)
            dve.wait_ge(wq_step, 11)
            dve.wait_ge(unit_done, PRO_UNITS + 1)
            nc.vector.tensor_tensor(ffn_q[:, :], ffn_q[:, :], ring[:, PRO_UNITS % 2, 0, 0:D], ALU.add).then_inc(unit_free, 1)

            def post(c, k, slot, u):
                base = DVE_POST * c
                dve.wait_ge(unit_done, u)
                if k < 2:
                    o = ring[:, slot, :, :].rearrange("p i (h r) -> p i h r", r=VW)
                    nc.vector.reciprocal(rsum[:, 2 * k:2 * k + 2, :], o[:, :, :, DK]).then_inc(dve_post, 1)
                    dve.wait_ge(dve_post, base + k + 1)
                    nc.vector.tensor_tensor(on[:, 2 * k:2 * k + 2, :].rearrange("p i (h d) -> p i h d", d=DK), o[:, :, :, 0:DK],
                                            rsum[:, 2 * k:2 * k + 2, :].rearrange("p i (h a) -> p i h a", a=1)
                                            .to_broadcast([128, 2, H, DK]), ALU.mult).then_inc(unit_free, 1)
                if k == 2:
                    nc.vector.tensor_copy(onT, ring[:, slot, 0, :]).then_inc(unit_free, 1)
                if k == 4:
                    nc.vector.tensor_copy(x1T, ring[:, slot, 0, :]).then_inc(unit_free, 1)
                if k in (3, 5):
                    at = base + DVE_ON + (1 if k == 3 else 1 + 2 * TPC)
                    added = x_sb[:, c * TPC:(c + 1) * TPC, :] if k == 3 else x1b[:, :, :]
                    if k == 3 and c > 0:
                        dve.wait_ge(normed, normed_count(c - 1, 1))
                    if k == 5:
                        dve.wait_ge(normed, normed_count(c, 0))
                        dve.wait_ge(pool_post, pool_count(c, 0) + 1)
                    nc.vector.tensor_tensor(res[:, :, :], ring[:, slot, 0, :].rearrange("p (t d) -> p t d", d=D), added,
                                            ALU.add).then_inc(unit_free, 1)
                    dve.wait_ge(unit_free, 2 + u)
                    for t in range(TPC):
                        nc.vector.bn_stats(stats[:, t, :], res[:, t, :]).then_inc(dve_post, 1)
                    for t in range(TPC):
                        dve.wait_ge(dve_post, at + t)
                        nc.vector.bn_aggr(mv[:, t, :], stats[:, t, :]).then_inc(dve_post, 1)

            def apply_norm(c, norm):
                dve.wait_ge(pool_post, pool_count(c, norm))
                if norm and c > 0:
                    dve.wait_ge(stored, 16 * c)
                for t in range(TPC):
                    nc.vector.tensor_scalar((y_sb if norm else x1)[:, t, :], res[:, t, :], mv[:, t, 0:1], rstd[:, t:t + 1],
                                            ALU.subtract, ALU.mult).then_inc(normed, 1)

            def body(g, last):
                u = 0
                for e in schedule(last):
                    if e[0] == "NORM":
                        apply_norm(e[1], e[2])
                    if e[0] == "A":
                        slot = (RING_0 + u) % 2
                        u += 1
                        row_max(e[2], e[3], slot, g * GROUP_UNITS + (RING_0 + u))
                        if e[3] == score_units(e[2])[-1]:
                            combine(e[2], g * GROUP_UNITS + (RING_0 + u))
                    if e[0] == "M":
                        slot = (RING_0 + u) % 2
                        u += 1
                        rows(e[2], slot, g * GROUP_UNITS + (RING_0 + u))
                    if e[0] == "POST":
                        slot = (RING_0 + u) % 2
                        u += 1
                        post(e[1], e[2], slot, RING_0 + (NG - 1) * GROUP_UNITS + u)

            groups(dve, body)

        @block.tensor
        def _(pe):
            pe.wait_ge(consts, 6)
            pe.wait_ge(ld_w, 48)
            bank = prep_begin(pe, ("W", 0))
            for w in range(3):
                nc.tensor.transpose(bank[:, w * 128:(w + 1) * 128], wqkv_sb[:, w, :], ident[:, :])
            nc.tensor.transpose(bank[:, 384:512], wo_sb[:, :], ident[:, :]).then_inc(bank_done[0], 1)
            bank = prep_begin(pe, ("L", 0))
            nc.tensor.transpose(bank[0:RANK, 0:128], a_sb[:, :], ident[:, :]).then_inc(bank_done[1], 1)

            def transpose_x(c):
                pe.wait_ge(ld_x[c], 16)
                bank = prep_begin(pe, ("X", c))
                for t in range(TPC):
                    last = nc.tensor.transpose(bank[:, t * TOK:(t + 1) * TOK], x_sb[:, c * TPC + t, :], ident[:, :])
                last.then_inc(bank_done[prep_bank_of(("X", c))[0]], 1)

            def prep(c):
                if c == 0:
                    transpose_x(0)
                    pe.wait_ge(w_done, 6)
                b, n = prep_bank_of(("X", c))
                pe.wait_ge(bank_free[b], n)
                for kind, w in (("Q", wT[:, 0, :]), ("QS", wTs[:, 0, :]), ("K", wT[:, 1, :]), ("KS", wTs[:, 1, :])):
                    bank = prep_begin(pe, (kind, c))
                    nc.tensor.matmul(bank, w, xT[:, c % 2, :], start=True, stop=True).then_inc(bank_done[prep_bank_of((kind, c))[0]], 1)
                if c + 1 < NC:
                    transpose_x(c + 1)
                bank = prep_begin(pe, ("V", c))
                for t in range(TPC):
                    last = nc.tensor.matmul(bank[:, t * D:(t + 1) * D], xT[:, c % 2, t * TOK:(t + 1) * TOK],
                                            wT[:, 2, :], start=True, stop=True)
                last.then_inc(bank_done[prep_bank_of(("V", c))[0]], 1)

            def scores(c, unit, slot, u_free):
                kk, ii, hp = unit
                w = CH if kk < c else (ii + 1) * TOK
                pe.wait_ge(unit_free, u_free)
                for i in range(2):
                    h = 2 * hp + i
                    dst = ring[:, slot, i, :]
                    last = nc.tensor.matmul(dst[:, 0:w], qA[:, c, h, ii * TOK:(ii + 1) * TOK], kA[:, kk, h, 0:w],
                                            start=True, stop=kk < c)
                    if kk == c:
                        last = nc.tensor.matmul(dst[:, w - TOK:w], ident_h[:, :], causal[:, :], start=False, stop=True)
                last.then_inc(unit_done, 1)

            def maxima_rows(c, slot, u_free, before, n):
                pe.wait_ge(unit_free, u_free)
                pe.wait_ge(nsplit, before * 4 + 4 * n)
                nc.tensor.transpose(ring[:, slot, 0, 0:TOK // 2].bitcast(bf16), nparts[:, c, :], ident_h[:, :]).then_inc(unit_done, 1)

            u, split = 0, 0
            for e in prologue():
                if e[0] == "P":
                    prep(e[1])
                if e[0] == "A":
                    if e[3] == (0, 0, 0):
                        pe.wait_ge(qkA_in[e[2]], 16 * N_A)
                    scores(e[2], e[3], u % 2, u + 1)
                    u += 1
                if e[0] == "M":
                    split += 1
                    maxima_rows(e[2], u % 2, u + 1, 0, split)
                    u += 1
            pe.wait_ge(unit_free, u + 1)
            pe.wait_ge(ld_ffn, 48)
            pe.wait_ge(bank_free[1], 1)
            nc.tensor.matmul(ring[:, u % 2, 0, 0:D], aT[:, :], b_sb[:, :], start=True, stop=True).then_inc(unit_done, 1)
            pe.sem_inc(probs_free, PRING)
            for b in range(4):
                pe.wait_ge(bank_free[b], (len(PREP) - b + 3) // 4)

            def post(c, k, slot, u_free):
                base = DVE_POST * c
                pe.wait_ge(unit_free, u_free)
                if k < 2:
                    pe.wait_ge(o_free, 1 + (NG - 1) * NC + c + 1)
                    for i in range(2):
                        t = c * TPC + 2 * k + i
                        for g in range(NG):
                            last = nc.tensor.transpose(ring[:, slot, i, g * 128:(g + 1) * 128],
                                                       oT[:, g, t * TOK:(t + 1) * TOK], ident[:, :])
                if k == 2:
                    pe.wait_ge(unit_free, u_free + 1)
                    for t in range(TPC):
                        last = nc.tensor.transpose(ring[:, slot, 0, t * TOK:(t + 1) * TOK], on[:, t, :], ident[:, :])
                if k == 3:
                    pe.wait_ge(unit_free, u_free + 1)
                    for t in range(TPC):
                        last = nc.tensor.matmul(ring[:, slot, 0, t * D:(t + 1) * D], onT[:, t * TOK:(t + 1) * TOK],
                                                wT[:, 3, :], start=True, stop=True)
                if k == 4:
                    pe.wait_ge(normed, normed_count(c, 0))
                    for t in range(TPC):
                        last = nc.tensor.transpose(ring[:, slot, 0, t * TOK:(t + 1) * TOK], x1[:, t, :], ident[:, :])
                if k == 5:
                    pe.wait_ge(unit_free, u_free + 1)
                    for t in range(TPC):
                        last = nc.tensor.matmul(ring[:, slot, 0, t * D:(t + 1) * D], x1T[:, t * TOK:(t + 1) * TOK],
                                                ffn_q[:, :], start=True, stop=True)
                last.then_inc(unit_done, 1)

            def body(g, last):
                u, split = 0, 2
                for e in schedule(last):
                    if e[0] in RING_EVENTS:
                        slot = (RING_0 + u) % 2
                        u_free = g * GROUP_UNITS + (RING_0 + u + 1)
                        u += 1
                    if e[0] == "A":
                        if e[3] == (0, 0, 0):
                            for k in (range(e[2] + 1) if not e[1] else [e[2]]):
                                pe.wait_ge(qkA_in[k], g * 16 * N_A + (1 + e[1]) * 16 * N_A)
                        scores(e[2], e[3], slot, u_free)
                    if e[0] == "M":
                        split += 1
                        maxima_rows(e[2], slot, u_free, g * 4, split)
                    if e[0] == "S":
                        c, j = e[1], e[2]
                        J = step_index(c, j)
                        lo = max(0, j - TPC * c) * TOK
                        if j == 0 and e[3] == 0:
                            pe.wait_ge(qkB_in[c], g * 32 + 32)
                            pe.wait_ge(mrow_in[c], g * 16 + 16)
                        for h in (2 * e[3], 2 * e[3] + 1):
                            n = J * HG + h
                            used = n + 1 if n >= SBANKS else SBANKS if n == 0 else n
                            pe.wait_ge(exp_done, g * BLOCKS + used)
                            nc.tensor.matmul(sT[:, n % SBANKS, lo:CH], kB[:, j // TPC, h, (j % TPC) * TOK:(j % TPC + 1) * TOK],
                                             qB[:, c, h, lo:CH], start=True, stop=True).then_inc(s_done, 1)
                    if e[0] == "PV":
                        c, j = e[1], e[2]
                        J = step_index(c, j)
                        lo = max(0, j - TPC * c) * TOK
                        if j == 0:
                            pe.wait_ge(o_free, g * NC + (c + 1))
                            pe.wait_ge(v_staged, g * NC + (4 + c + 1))
                        if j >= TPC * c:
                            pe.wait_ge(masked, g * (NC * TPC) + (j + 1))
                        else:
                            pe.wait_ge(exp_done, g * BLOCKS + (SBANKS + (J + 1) * HG))
                        for h in range(HG):
                            last_pv = nc.tensor.matmul(oP[VW * h:VW * (h + 1), lo:CH], v_g[:, j, h, :],
                                                       probs[:, J % PRING, h, lo:CH], start=j == 0,
                                                       stop=j == TPC * (c + 1) - 1)
                        last_pv.then_inc(probs_free, 1)
                    if e[0] == "POST":
                        post(e[1], e[2], slot, u_free)

            groups(pe, body)


_INS = ['L0_attn_x', 'L0_attn_W_qkv', 'L0_attn_W_o', 'L0_ffn_kernel', 'L0_ffn_bias', 'L0_ffn_a', 'L0_ffn_b']
_OUTS = [((1, S, D), 'float32')]


def kernel(**inputs):
    import numpy as _np
    import concourse.bacc as _bacc
    from concourse import mybir as _mybir
    from concourse.bass_utils import run_bass_kernel_spmd as _run

    nc = _bacc.Bacc("TRN2", target_bir_lowering=False, num_devices=1)
    arrays, args = {}, []
    for name in _INS:
        a = _np.ascontiguousarray(inputs[name])
        arrays[f"in_{name}_dram"] = a
        args.append(nc.dram_tensor(f"in_{name}_dram", a.shape, _mybir.dt.from_np(a.dtype), kind="ExternalInput").ap())
    tables = rope_tables()
    arrays["rope_tables_dram"] = tables
    args.append(nc.dram_tensor("rope_tables_dram", tables.shape, _mybir.dt.from_np(tables.dtype), kind="ExternalInput").ap())
    for i, (shape, dtype) in enumerate(_OUTS):
        dt = _mybir.dt.from_np(_np.dtype(dtype))
        args.append(nc.dram_tensor(f"out_{i}_dram", shape, dt, kind="ExternalOutput").ap())
    attention_block(nc, *args)
    r = _run(nc, [arrays], core_ids=[0])
    got = tuple(r.results[0][f"out_{i}_dram"] for i in range(len(_OUTS)))
    return got[0]
```

```python
import numpy as np
import concourse.bass as bass
from concourse import mybir
from contextlib import ExitStack

S, D, H, DK = 2048, 128, 16, 8
RANK = 16
THETA = 10000.0
TOK = 128
CH = 512
NT, NC, TPC = S // TOK, S // CH, CH // TOK
HG = 4
NG = H // HG
PARTS = 3
TERMS = PARTS * PARTS * DK
SHIFT_ROW = 96
KROWS = 128
VW = 32
SBANKS = 3
PRING = 4
NEG = -3.0e38
EPS = 1e-5
ONE_PAIR = 1.0 + 0x3F80 / 2 ** 23


def rope_tables():
    inv = np.float32(THETA) ** (-np.arange(0, DK, 2, dtype=np.float32) / np.float32(DK))
    ang = np.arange(S, dtype=np.float32)[None, :] * inv.astype(np.float32)[:, None]
    cos = np.repeat(np.cos(ang), 2, axis=0)
    sin = np.repeat(np.sin(ang), 2, axis=0)
    sin[0::2] *= -1
    rows = [np.tile(np.repeat(t, HG, axis=0), (NG, 1)) for t in (cos, sin)]
    return np.ascontiguousarray(np.stack(rows).astype(np.float32))


def score_units(c):
    return [(kk, ii, hp) for kk in range(c + 1) for ii in range(TPC) for hp in range(HG // 2)]


def pace(work, weights, cost):
    total, whole = sum(cost(w) for w in work), sum(weights)
    out, spent, at, passed = [], 0.0, 0, 0.0
    for w in weights:
        passed += w
        here = []
        while at < len(work) and spent + 0.5 * cost(work[at]) <= total * passed / whole + 1e-6:
            here.append(work[at])
            spent += cost(work[at])
            at += 1
        out.append(here)
    out[-1] += work[at:]
    return out


def reduce_cost(e):
    if e[0] != "A":
        return 0.0
    kk, ii, _ = e[3]
    return 64 + 2 * (CH if kk < e[2] else (ii + 1) * TOK)


def maxima_order(nxt, c, units, after):
    return (units + after[:2] + [("N", nxt, c)] + after[2:6] + [("M", nxt, c)] + after[6:])


AHEAD = 3 * TPC


def early_units(nxt):
    zero, one, two = ([("A", nxt, c, u) for u in score_units(c)] for c in range(3))
    return maxima_order(nxt, 0, zero, maxima_order(nxt, 1, one, two[:AHEAD]))


def schedule(part):
    first, last = part == "first", part == "last"
    steps = [(c, j) for c in range(NC) for j in range(TPC * (c + 1))]
    weight = {(c, j): min(1.0, (TPC * (c + 1) - j) / TPC) for c, j in steps}
    post = {}
    if last:
        for c in range(NC - 1):
            for e, at in zip(POST_ORDER, POST_STEPS[c]):
                post.setdefault(steps[step_index(c + 1, 0) + at], []).append((e[0], c, e[1]))
    main, pv = [], []
    for c, j in steps:
        main.append(([("S", c, j, 0)], FILL[0] * weight[c, j]))
        if len(pv) > 1:
            main.append(([("PV",) + pv[0]], FILL[1] * weight[pv.pop(0)]))
        main.append(([("S", c, j, 1)] + post.get((c, j), []), FILL[2] * weight[c, j]))
        pv.append((c, j))
    main += [([("PV",) + p], FILL[1] * weight[p]) for p in pv]
    early = [] if last else early_units(1)
    third = maxima_order(0, 3, [("A", 0, 3, u) for u in score_units(3)], early)
    if first:
        zero, one, two = ([("A", 0, c, u) for u in score_units(c)] for c in range(3))
        second = maxima_order(0, 1, one, maxima_order(0, 2, two, third))
        second.insert(second.index(("M", 1, 0)) + 1, ("L",))
        ahead = [("P", 0), ("D", 0), ("P", 1), ("D", 1), ("P", 2), ("D", 2)] + zero \
            + [("N", 0, 0), ("P", 3), second[0], ("M", 0, 0), ("D", 3)] + second[1:8]
        work, cuts = second[8:], (1, 2, 3)
    else:
        two = [("A", 0, 2, u) for u in score_units(2)[AHEAD:]]
        ahead, work, cuts = [], maxima_order(0, 2, two, third), (3,)
    fill, at = [], 0
    for c in cuts:
        due = next(i for i, (es, _) in enumerate(main) if es[0] == ("S", c, 0, 0)) - DUE
        n = work.index(("M", 0, c)) + 1
        if last:
            work.pop(n - 1)
            main[due][0].append(("M", 0, c))
            n, due = n - 1, due - GAP
        fill += pace(work[:n], [w for _, w in main[at:due]], reduce_cost)
        work, at = work[n:], due
    fill += pace(work, [w for _, w in main[at:]], reduce_cost)
    out = ahead
    for (es, _), work in zip(main, fill):
        out += es + work
    if last:
        out += [(e[0], NC - 1, e[1]) for e in POST_ORDER]
    return out


POST_ORDER = (("POST", 0), ("POST", 1), ("POST", 2), ("POST", 3), ("NORM", 0), ("POST", 4), ("POST", 5), ("NORM", 1))
POST_STEPS = [(3, 4, 6, 8, 10, 11, 13, 15), (10, 11, 12, 13, 15, 15, 16, 18), (6, 7, 8, 9, 11, 11, 12, 14)]


def step_index(c, j):
    return sum(TPC * (b + 1) for b in range(c)) + j


FILL = (0.4, 1.4, 2)
DUE = 5
GAP = 2
RING_EVENTS = ("A", "M", "L", "POST")
FIRST_UNITS, GROUP_UNITS = (sum(e[0] in RING_EVENTS for e in schedule(part)) for part in ("first", "middle"))
STEPS = sum(TPC * (c + 1) for c in range(NC))
BLOCKS = STEPS * HG


def attention_block(nc, x, w_qkv, w_o, ffn_w, ffn_bias, lora_a, lora_b, tables, out):
    fp32, bf16 = mybir.dt.float32, mybir.dt.bfloat16
    ALU, ACT, AX = mybir.AluOpType, mybir.ActivationFunctionType, mybir.AxisListType
    absmax = bass.bass_isa.ReduceOp.absmax

    x_t = x.rearrange("a (t p) d -> p (a t) d", p=TOK)
    out_t = out.rearrange("a (t p) d -> p (a t) d", p=TOK)

    ctx = ExitStack()
    with ctx:
        def sb(name, shape, dt=fp32):
            return ctx.enter_context(nc.sbuf_tensor(name, shape, dt))

        def sem(name):
            return ctx.enter_context(nc.semaphore(name))

        x_sb = sb("x_sb", [128, NT, D])
        wqkv_sb = sb("wqkv_sb", [128, 3, D])
        wo_sb = sb("wo_sb", [128, D])
        ffn_sb = sb("ffn_sb", [128, D])
        a_sb = sb("a_sb", [128, RANK])
        b_sb = sb("b_sb", [RANK, D])
        bias_sb = sb("bias_sb", [128, D])
        ident = sb("ident", [128, 128])
        ident_h = sb("ident_h", [128, 128], bf16)
        causal = sb("causal", [128, 128], bf16)
        wT = sb("wT", [128, 4, D])
        wTs = sb("wTs", [128, 2, D])
        aT = sb("aT", [RANK, 128])
        ffn_q = sb("ffn_q", [128, D])
        wst = sb("wst", [128, 8])
        rot = sb("rot", [128, 2, 3, CH])
        qp = sb("qp", [128, 2, PARTS, CH], bf16)
        kp = sb("kp", [128, 2, PARTS, CH], bf16)
        q_dram = nc.dram_tensor("q_parts", [NC, PARTS, NG, DK * HG, CH], bf16, kind="Internal").ap()
        k_dram = nc.dram_tensor("k_parts", [NC, PARTS, NG, DK * HG, CH], bf16, kind="Internal").ap()
        v_all = sb("v_all", [128, NT, H, DK])
        qA = sb("qA", [128, NC, HG, CH], bf16)
        kA = sb("kA", [128, NC, HG, CH], bf16)
        qB = sb("qB", [128, NC, HG, CH], bf16)
        kB = sb("kB", [128, NC, HG, CH], bf16)
        v_g = sb("v_g", [128, NT, HG, VW])
        pmax = sb("pmax", [128, NC, HG, TPC, NC])
        nmax = sb("nmax", [128, NC, HG * TPC])
        nrest = sb("nrest", [128, NC, HG * TPC])
        nparts = sb("nparts", [128, NC, 128], bf16)
        mrows = sb("mrows", [PARTS * HG * TPC, NC, TOK], bf16)
        probs = sb("probs", [128, PRING, HG, CH])
        xT = probs[:, 0, 0:2, :]
        cs_sb = [probs[:, 1 + c // 2, 2 * (c % 2):2 * (c % 2) + 2, :] for c in range(NC)]
        oT = sb("oT", [128, NG, S])
        rsum = sb("rsum", [128, TPC, H])
        on, res, x1 = (rot[:, 0, i, :].rearrange("p (t d) -> p t d", d=D) for i in range(3))
        onT, x1T = rot[:, 1, 0, :], rot[:, 1, 1, :]
        x1b = rot[:, 1, 2, :].rearrange("p (t d) -> p t d", d=D)
        stats = sb("stats", [128, TPC, 6])
        mv = sb("mv", [128, TPC, 2])
        rstd = sb("rstd", [128, TPC])
        mhalf = sb("mhalf", [128, TPC])
        y_sb = sb("y_sb", [128, TPC, D])

        ring = ctx.enter_context(nc.psum_tensor("ring", [128, 2, 2, CH], fp32))
        sT = ctx.enter_context(nc.psum_tensor("sT", [128, SBANKS, CH], fp32))
        oP = ctx.enter_context(nc.psum_tensor("oP", [128, CH], fp32))
        prep_bank = [sT[:, 0, :], sT[:, 1, :], sT[:, 2, :], oP[:, :]]

        ld_w = sem("ld_w")
        ld_ffn = sem("ld_ffn")
        ld_x = [sem(f"ld_x{c}") for c in range(NC)]
        ld_cs = [sem(f"ld_cs{c}") for c in range(NC)]
        consts = sem("consts")
        filled = sem("filled")
        filled_b = sem("filled_b")
        bank_done = [sem(f"bank_done{b}") for b in range(4)]
        bank_free = [sem(f"bank_free{b}") for b in range(4)]
        rope_sum, part_done, rest_done = ([sem(f"{n}_{w}") for w in "qk"] for n in ("rope_sum", "part_done", "rest_done"))
        w_done = sem("w_done")
        wq_step = sem("wq_step")
        parts_out = [[sem(f"{w}parts_out{c}") for w in "qk"] for c in range(NC)]
        qkA_in = [sem(f"qkA_in{c}") for c in range(NC)]
        qkB_in = [sem(f"qkB_in{c}") for c in range(NC)]
        unit_done = sem("unit_done")
        unit_free = sem("unit_free")
        nmax_done = sem("nmax_done")
        nsplit = sem("nsplit")
        mrow_in = [sem(f"mrow_in{c}") for c in range(NC)]
        s_done = sem("s_done")
        exp_done = sem("exp_done")
        masked = sem("masked")
        gate = sem("gate")
        probs_free = sem("probs_free")
        o_free = sem("o_free")
        v_staged = sem("v_staged")
        dve_post = sem("dve_post")
        pool_post = sem("pool_post")
        normed = sem("normed")
        stored = sem("stored")

        block = ctx.enter_context(nc.Block())

        def groups(eng, body):
            body(0, "first")
            with eng.Fori(1, NG - 1) as g:
                body(g, "middle")
            body(NG - 1, "last")

        def ring_unit(g, part, u):
            return u if part == "first" else g * GROUP_UNITS + (FIRST_UNITS - GROUP_UNITS + u)

        def ring_slot(part, u):
            return (u if part == "first" else FIRST_UNITS - GROUP_UNITS + u) % 2

        PREP = [("W", 0), ("L", 0)]
        PREP += [("X", 0)]
        for c in range(NC):
            PREP += [(k, c) for k in ("Q", "QS", "K", "KS")] + ([("X", c + 1)] if c < NC - 1 else []) + [("V", c)]
        PREP_AT = {u: n for n, u in enumerate(PREP)}

        def prep_bank_of(u):
            return PREP_AT[u] % 4, PREP_AT[u] // 4 + 1

        def prep_begin(pe, u):
            b, n = prep_bank_of(u)
            if n > 1:
                pe.wait_ge(bank_free[b], n - 1)
            return prep_bank[b]

        def prep_read(eng, u):
            b, n = prep_bank_of(u)
            eng.wait_ge(bank_done[b], n)
            return prep_bank[b]

        def store_parts(sp, c):
            for w, (parts, dram) in enumerate(((qp, q_dram), (kp, k_dram))):
                sp.wait_ge(part_done[w], 2 * (c + 1))
                sp.wait_ge(rest_done[w], 2 * (c + 1))
                sp.dma_start(dram[c, :, :, :, :].rearrange("a g r s -> (g r) a s"), parts[:, c % 2, :, :]).then_inc(parts_out[c][w], 16)

        N_A = 2 * PARTS

        def load_A(sp, c, g, first=False):
            for w, (operand, dram) in enumerate(((qA, q_dram), (kA, k_dram))):
                if first:
                    sp.wait_ge(parts_out[c][w], 16)
                for a in range(PARTS):
                    rows = operand[a * PARTS * DK:(a + 1) * PARTS * DK, c, :, :].rearrange("r h s -> r (h s)")
                    if w == 0:
                        part = dram[c, a, bass.ds(g, 1), :, :].rearrange("x (d h) s -> x d (h s)", h=HG)\
                            .to_broadcast([PARTS, DK, HG * CH])
                    else:
                        part = dram[c, :, bass.ds(g, 1), :, :].rearrange("b x (d h) s -> b (x d) (h s)", h=HG)
                    sp.dma_start(rows, part).then_inc(qkA_in[c], 16)

        def load_B(sp, c):
            sp.dma_start(qB[0:TERMS, c, :, :], qA[0:TERMS, c, :, :]).then_inc(qkB_in[c], 16)
            sp.dma_start(kB[0:TERMS, c, :, :], kA[0:TERMS, c, :, :]).then_inc(qkB_in[c], 16)

        def load_maxima(sp, c, u_free):
            sp.wait_ge(unit_free, u_free)
            sp.dma_start(qB[SHIFT_ROW:SHIFT_ROW + PARTS, c, :, :], mrows[:, c, :]).then_inc(mrow_in[c], 16)

        POOL_1, POOL_2 = 3, 2

        def pool_count(c, norm):
            return c * (POOL_1 + POOL_2) + (POOL_1 + POOL_2 if norm else 2)

        def normed_count(c, norm):
            return (2 * c + norm + 1) * TPC

        DVE_ON = 2
        DVE_POST = DVE_ON + 2 * (2 * TPC)

        @block.sync
        def _(sp):
            sp.dma_start(x_sb[:, 0:TPC, :], x_t[:, 0:TPC, :]).then_inc(ld_x[0], 16)
            sp.dma_start(wqkv_sb[:, :, :], w_qkv.rearrange("(k p) d -> p k d", p=128)).then_inc(ld_w, 16)
            sp.dma_start(wo_sb[:, :], w_o).then_inc(ld_w, 16)
            sp.dma_start(a_sb[:, :], lora_a).then_inc(ld_w, 16)
            for c in range(NC):
                sp.dma_start(cs_sb[c],
                             tables[:, :, c * CH:(c + 1) * CH].rearrange("w p s -> p w s")).then_inc(ld_cs[c], 16)
            for c in range(1, NC):
                sp.dma_start(x_sb[:, c * TPC:(c + 1) * TPC, :], x_t[:, c * TPC:(c + 1) * TPC, :]).then_inc(ld_x[c], 16)
            sp.dma_start(ffn_sb[:, :], ffn_w).then_inc(ld_ffn, 16)
            sp.dma_start(b_sb[:, :], lora_b).then_inc(ld_ffn, 16)
            sp.dma_start(bias_sb[:, :], ffn_bias.rearrange("(a n) -> a n", a=1).to_broadcast([128, D])).then_inc(ld_ffn, 16)
            sp.wait_ge(filled, 2)
            def body(g, part):
                u, last = 0, part == "last"
                for e in schedule(part):
                    u += e[0] in RING_EVENTS
                    if e[0] == "D":
                        c = e[1]
                        store_parts(sp, c)
                        load_A(sp, c, 0, True)
                        if c == 1:
                            sp.wait_ge(filled_b, 3)
                        for b in ([c - 1] if c == 1 or c == 2 else [c - 1, c] if c == 3 else []):
                            sp.wait_ge(qkA_in[b], 16 * N_A)
                            load_B(sp, b)
                    if e[0] == "M":
                        load_maxima(sp, e[2], ring_unit(g, part, 2 + u))
                    free = None
                    if e[0] == "A" and e[2] == 3 and e[3][1:] == (TPC - 1, HG // 2 - 1) and e[3][0] < NC - 1:
                        free = e[3][0]
                    if e[0] == "M" and e[2] == NC - 1:
                        free = NC - 1
                    if free is not None and not last:
                        sp.wait_ge(unit_done, ring_unit(g, part, u))
                        sp.wait_ge(qkB_in[free], g * 32 + 32)
                        load_A(sp, free, g + 1)
                    if e[0] == "S" and not last and e[1] == NC - 1 and e[3] == 1 and e[2] % TPC == TPC - 1:
                        c = e[2] // TPC
                        sp.wait_ge(s_done, g * BLOCKS + (step_index(NC - 1, e[2]) + 1) * HG)
                        sp.wait_ge(qkA_in[c], g * 16 * N_A + 2 * 16 * N_A)
                        load_B(sp, c)
                    if e[0] == "NORM" and e[2] == 1:
                        c = e[1]
                        sp.wait_ge(normed, normed_count(c, 1))
                        sp.dma_start(out_t[:, c * TPC:(c + 1) * TPC, :], y_sb[:, :, :]).then_inc(stored, 16)

            groups(sp, body)
            sp.wait_ge(stored, 16 * NC)

        def stage_v(pool, c, g):
            tiles = slice(c * TPC, (c + 1) * TPC)
            nc.gpsimd.tensor_copy(v_g[:, tiles, :, 0:DK], v_all[:, tiles, bass.ds(g * HG, HG), :]).then_inc(v_staged, 1)

        def add_rotation(eng, ops, c, w):
            for kind in (("Q", "QS"), ("K", "KS"))[w]:
                b, uses = prep_bank_of((kind, c))
                eng.wait_ge(bank_free[b], uses)
            if c > 0:
                eng.wait_ge(rest_done[w], 2 * c)
            ops.tensor_tensor(rot[:, w, 2, :], rot[:, w, 0, :], rot[:, w, 1, :], ALU.add).then_inc(rope_sum[w], 1)

        def split_rotation(eng, ops, c, w, parts):
            eng.wait_ge(rope_sum[w], c + 1)
            eng.wait_ge(part_done[w], 2 * c + 1)
            ops.tensor_tensor(rot[:, w, 2, :], rot[:, w, 2, :], parts[:, c % 2, 0, :], ALU.subtract).then_inc(rest_done[w], 1)
            eng.wait_ge(rest_done[w], 2 * c + 1)
            eng.wait_ge(part_done[w], 2 * c + 2)
            ops.tensor_tensor(parts[:, c % 2, 2, :], rot[:, w, 2, :], parts[:, c % 2, 1, :], ALU.subtract).then_inc(rest_done[w], 1)

        def stage_v_in(pool, c):
            b, uses = prep_bank_of(("V", c))
            pool.wait_ge(bank_free[b], uses)
            pool.wait_ge(v_staged, 4)
            stage_v(pool, c, 0)

        def split_maxima(pool, c, before, n):
            n_m = HG * TPC
            part = [nparts[:, c, a * n_m:(a + 1) * n_m] for a in range(PARTS)]
            pool.wait_ge(nmax_done, before + n)
            pool.sem_inc(gate, 1)
            nc.gpsimd.tensor_copy(part[0], nmax[:, c, :]).then_inc(nsplit, 1)
            pool.wait_ge(nsplit, before * 4 + (4 * n - 3))
            nc.gpsimd.tensor_tensor(nrest[:, c, :], nmax[:, c, :], part[0], ALU.subtract).then_inc(nsplit, 1)
            pool.wait_ge(nsplit, before * 4 + (4 * n - 2))
            pool.sem_inc(gate, 1)
            nc.gpsimd.tensor_copy(part[1], nrest[:, c, :]).then_inc(nsplit, 1)
            pool.wait_ge(nsplit, before * 4 + (4 * n - 1))
            nc.gpsimd.tensor_tensor(part[2], nrest[:, c, :], part[1], ALU.subtract).then_inc(nsplit, 1)

        def post_rstd(pool, c, norm):
            base = pool_count(c, norm) - 2
            pool.wait_ge(dve_post, DVE_POST * c + DVE_ON + (norm + 1) * 2 * TPC)
            nc.gpsimd.tensor_scalar(rstd[:, :], mv[:, :, 1], EPS, None, ALU.add).then_inc(pool_post, 1)
            pool.wait_ge(pool_post, base + 1)
            nc.gpsimd.tensor_tensor(rstd[:, :], rstd[:, :], mhalf[:, :], ALU.pow).then_inc(pool_post, 1)

        def post_bias(pool, c):
            pool.wait_ge(normed, normed_count(c, 0))
            nc.gpsimd.tensor_tensor(x1b[:, :, :], x1[:, :, :],
                                    bias_sb[:, :].rearrange("p (a d) -> p a d", a=1).to_broadcast([128, TPC, D]),
                                    ALU.add).then_inc(pool_post, 1)

        def weight_scale(pool):
            pool.wait_ge(ld_ffn, 48)
            pool.wait_ge(wq_step, 1)
            nc.gpsimd.partition_all_reduce(wst[:, 1:2], wst[:, 0:1], 128, absmax).then_inc(wq_step, 1)
            for n, (o, a, k, b, op) in enumerate(((2, 1, 1.0 / 7.0, None, None), (4, 2, 8.0, 1, ALU.subtract), (4, 2, 1.0, 4, ALU.subtract),
                                                  (4, 4, 1.0 / 7.0, 2, ALU.add))):
                pool.wait_ge(wq_step, n + 2)
                if b is None:
                    nc.gpsimd.tensor_scalar(wst[:, o:o + 1], wst[:, a:a + 1], k, None, ALU.mult).then_inc(wq_step, 1)
                else:
                    nc.gpsimd.tensor_scalar(wst[:, o:o + 1], wst[:, a:a + 1], k, wst[:, b:b + 1], ALU.mult, op).then_inc(wq_step, 1)

        @block.gpsimd
        def _(pool):
            pool.memset(ident[:, :], 0.0).then_inc(consts, 1)
            pool.memset(ident_h[:, :], 0.0).then_inc(consts, 1)
            pool.memset(causal[:, :], 0.0).then_inc(consts, 1)
            pool.wait_ge(consts, 3)
            for m in (ident, ident_h):
                pool.affine_select(out=m[:, :], in_=m[:, :], compare_op=ALU.not_equal, fill=1.0, base=0,
                                   pattern=[[-1, 128]], channel_multiplier=1).then_inc(consts, 1)
            pool.affine_select(out=causal[:, :], in_=causal[:, :], compare_op=ALU.is_ge, fill=NEG, base=0,
                               pattern=[[-1, 128]], channel_multiplier=1).then_inc(consts, 1)
            pool.memset(v_g[:, :, :, :], 0.0).then_inc(v_staged, 1)
            pool.wait_ge(v_staged, 1)
            pool.memset(v_g[:, :, :, DK:DK + 1], 1.0).then_inc(v_staged, 1)
            pool.memset(mhalf[:, :], -0.5).then_inc(v_staged, 1)
            pool.memset(nparts[:, :, :], 0.0).then_inc(v_staged, 1)
            pool.wait_ge(v_staged, 4)
            pool.memset(kB[64:96, :, :, :].bitcast(fp32), 0.0).then_inc(filled_b, 1)
            pool.wait_ge(filled_b, 1)
            pool.memset(kB[96:128, :, :, :].bitcast(fp32), ONE_PAIR).then_inc(filled_b, 1)
            pool.wait_ge(filled_b, 2)
            pool.memset(qB[64:128, :, :, :].bitcast(fp32), 0.0).then_inc(filled_b, 1)
            pool.wait_ge(filled_b, 3)
            def body(g, part):
                n_split, last = 0 if part == "first" else 2, part == "last"
                for e in schedule(part):
                    if e[0] == "P":
                        c = e[1]
                        for w, parts in ((0, qp), (1, kp)):
                            if w == 1 or c == NC - 1:
                                add_rotation(pool, nc.gpsimd, c, w)
                                split_rotation(pool, nc.gpsimd, c, w, parts)
                        stage_v_in(pool, c)
                    if part == "first" and e == ("M", 0, 2):
                        weight_scale(pool)
                    if e[0] == "S" and e[3] == 1 and e[2] >= TPC * e[1]:
                        c, jj = e[1], e[2] - TPC * e[1]
                        J = step_index(c, e[2])
                        pool.wait_ge(exp_done, g * BLOCKS + (SBANKS + (J + 1) * HG))
                        pool.sem_inc(gate, 1)
                        p = probs[:, J % PRING, :, jj * TOK:(jj + 1) * TOK]
                        pool.affine_select(out=p, in_=p, compare_op=ALU.is_ge, fill=0.0, base=0,
                                           pattern=[[0, HG], [1, TOK]], channel_multiplier=-1).then_inc(masked, 1)
                    if e[0] == "N":
                        n_split = n_split + 1
                        split_maxima(pool, e[2], g * 4, n_split)
                    if e[0] == "PV" and not last and e[1] == NC - 1 and e[2] % TPC == TPC - 1:
                        c = e[2] // TPC
                        pool.wait_ge(probs_free, g * STEPS + (PRING + step_index(NC - 1, e[2]) + 1))
                        pool.sem_inc(gate, 1)
                        stage_v(pool, c, g + 1)
                    if e[0] == "POST" and e[2] in (3, 5):
                        post_rstd(pool, e[1], 0 if e[2] == 3 else 1)
                    if e[0] == "NORM" and e[2] == 0:
                        post_bias(pool, e[1])

            groups(pool, body)

        @block.scalar
        def _(act):
            def evac(u, dst, src_of, done=None):
                src = prep_read(act, u)
                ins = nc.scalar.copy(dst, src_of(src))
                ins.then_inc(bank_free[prep_bank_of(u)[0]], 1)

            src = prep_read(act, ("W", 0))
            for w in range(2):
                nc.scalar.copy(wT[:, w, :].rearrange("p (g d h) -> p g h d", g=NG, d=DK),
                               src[:, w * D:(w + 1) * D].rearrange("p (g h d) -> p g h d", g=NG, d=DK)).then_inc(w_done, 1)
            nc.scalar.copy(wT[:, 2:4, :], src[:, 2 * D:4 * D].rearrange("p (w d) -> p w d", w=2)).then_inc(bank_free[0], 1)
            act.wait_ge(w_done, 2)
            for w in range(2):
                src = wT[:, w, :].rearrange("p (n e h) -> p n e h", e=2, h=HG)
                dst = wTs[:, w, :].rearrange("p (n e h) -> p n e h", e=2, h=HG)
                for e in range(2):
                    nc.scalar.copy(dst[:, :, e, :], src[:, :, 1 - e, :]).then_inc(w_done, 1)
            evac(("L", 0), aT[:, :], lambda s: s[0:RANK, 0:128])
            evac(("X", 0), xT[:, 0, :], lambda s: s)
            act.sem_inc(exp_done, SBANKS)
            act.sem_inc(o_free, 1)

            def prep(c):
                for w, parts in ((0, qp), (1, kp)):
                    if c >= 2:
                        act.wait_ge(parts_out[c - 2][w], 16)
                    act.wait_ge(rope_sum[w], c + 1)
                    nc.scalar.copy(parts[:, c % 2, 0, :], rot[:, w, 2, :]).then_inc(part_done[w], 1)
                    if w == 0 and c + 1 < NC:
                        if c > 0:
                            b, n = prep_bank_of(("V", c - 1))
                            act.wait_ge(bank_done[b], n)
                        evac(("X", c + 1), xT[:, (c + 1) % 2, :], lambda s: s)
                    if w == 1:
                        src = prep_read(act, ("V", c))
                        b = prep_bank_of(("V", c))[0]
                        nc.scalar.copy(v_all[:, c * TPC:(c + 1) * TPC, :, :],
                                       src.rearrange("p (t h d) -> p t h d", t=TPC, h=H)).then_inc(bank_free[b], 1)
                    act.wait_ge(rest_done[w], 2 * c + 1)
                    nc.scalar.copy(parts[:, c % 2, 1, :], rot[:, w, 2, :]).then_inc(part_done[w], 1)

            def flush_o(g, c):
                act.wait_ge(probs_free, g * STEPS + (PRING + step_index(c, TPC * (c + 1) - 1) + 1))
                nc.scalar.copy(oT[:, bass.ds(g, 1), c * CH:(c + 1) * CH],
                               oP[:, :].rearrange("p (a s) -> p a s", a=1)).then_inc(o_free, 1)

            def body(g, part):
                for e in schedule(part):
                    if e[0] == "P":
                        prep(e[1])
                    if e[0] == "S":
                        c, j = e[1], e[2]
                        J = step_index(c, j)
                        lo = max(0, j - TPC * c) * TOK
                        act.wait_ge(probs_free, g * STEPS + (J + 1))
                        for h in (2 * e[3], 2 * e[3] + 1):
                            act.wait_ge(s_done, g * BLOCKS + (J * HG + h + 1))
                            nc.scalar.activation(probs[:, J % PRING, h, lo:CH], sT[:, (J * HG + h) % SBANKS, lo:CH], ACT.Exp,
                                                 scale=float(DK) ** -0.5).then_inc(exp_done, 1)
                    if e[0] == "PV" and e[2] == TPC * (e[1] + 1) - 1:
                        flush_o(g, e[1])

            groups(act, body)

        @block.vector
        def _(dve):
            nc.vector.memset(qA[64:128, :, :, :].bitcast(fp32), 0.0).then_inc(filled, 1)
            nc.vector.memset(kA[64:128, :, :, :].bitcast(fp32), 0.0).then_inc(filled, 1)
            dve.sem_inc(unit_free, 2)

            def rotate(c):
                dve.wait_ge(ld_cs[c], 16)
                for w, names in ((0, ("Q", "QS")), (1, ("K", "KS"))):
                    if c > 0:
                        dve.wait_ge(rope_sum[w], c)
                    for i, kind in enumerate(names):
                        src = prep_read(dve, (kind, c))
                        b = prep_bank_of((kind, c))[0]
                        nc.vector.tensor_tensor(rot[:, w, i, :], src, cs_sb[c][:, i, :], ALU.mult).then_inc(bank_free[b], 1)
                    if w == 0 and c < NC - 1:
                        add_rotation(dve, nc.vector, c, 0)
                if c < NC - 1:
                    split_rotation(dve, nc.vector, c, 0, qp)

            def row_max(c, unit, slot, u):
                kk, ii, hp = unit
                w = CH if kk < c else (ii + 1) * TOK
                dve.wait_ge(unit_done, u)
                nc.vector.tensor_reduce(pmax[:, c, 2 * hp:2 * hp + 2, ii, kk], ring[:, slot, :, 0:w],
                                        AX.X, ALU.max).then_inc(unit_free, 1)

            def combine(c, u):
                dve.wait_ge(unit_free, 2 + u)
                nc.vector.tensor_reduce(nmax[:, c, :], pmax[:, c, :, :, 0:c + 1].rearrange("p h i k -> p (h i) k"),
                                        AX.X, ALU.max, negate=True).then_inc(nmax_done, 1)

            def rows(c, slot, u):
                dve.wait_ge(unit_done, u)
                nc.vector.tensor_copy(mrows[:, c, :], ring[0:PARTS * HG * TPC, slot, 0, 0:TOK // 2].bitcast(bf16)).then_inc(unit_free, 1)

            def quantise(slot, u):
                dve.wait_ge(wq_step, 6)
                nc.vector.reciprocal(wst[:, 3:4], wst[:, 4:5]).then_inc(wq_step, 1)
                dve.wait_ge(wq_step, 7)
                nc.vector.tensor_scalar(ffn_q[:, :], ffn_sb[:, :], wst[:, 3:4], None, ALU.mult).then_inc(wq_step, 1)
                dve.wait_ge(wq_step, 8)
                nc.vector.tensor_scalar(ffn_q[:, :], ffn_q[:, :], 12582912.0, 12582912.0, ALU.add, ALU.subtract).then_inc(wq_step, 1)
                dve.wait_ge(wq_step, 9)
                nc.vector.tensor_scalar(ffn_q[:, :], ffn_q[:, :], -8.0, 7.0, ALU.max, ALU.min).then_inc(wq_step, 1)
                dve.wait_ge(wq_step, 10)
                nc.vector.tensor_scalar(ffn_q[:, :], ffn_q[:, :], wst[:, 4:5], None, ALU.mult).then_inc(wq_step, 1)
                dve.wait_ge(wq_step, 11)
                dve.wait_ge(unit_done, u)
                nc.vector.tensor_tensor(ffn_q[:, :], ffn_q[:, :], ring[:, slot, 0, 0:D], ALU.add).then_inc(unit_free, 1)

            def post(c, k, slot, u):
                base = DVE_POST * c
                dve.wait_ge(unit_done, u)
                if k < 2:
                    o = ring[:, slot, :, :].rearrange("p i (h r) -> p i h r", r=VW)
                    nc.vector.reciprocal(rsum[:, 2 * k:2 * k + 2, :], o[:, :, :, DK]).then_inc(dve_post, 1)
                    dve.wait_ge(dve_post, base + k + 1)
                    nc.vector.tensor_tensor(on[:, 2 * k:2 * k + 2, :].rearrange("p i (h d) -> p i h d", d=DK), o[:, :, :, 0:DK],
                                            rsum[:, 2 * k:2 * k + 2, :].rearrange("p i (h a) -> p i h a", a=1)
                                            .to_broadcast([128, 2, H, DK]), ALU.mult).then_inc(unit_free, 1)
                if k == 2:
                    nc.vector.tensor_copy(onT, ring[:, slot, 0, :]).then_inc(unit_free, 1)
                if k == 4:
                    nc.vector.tensor_copy(x1T, ring[:, slot, 0, :]).then_inc(unit_free, 1)
                if k in (3, 5):
                    at = base + DVE_ON + (1 if k == 3 else 1 + 2 * TPC)
                    added = x_sb[:, c * TPC:(c + 1) * TPC, :] if k == 3 else x1b[:, :, :]
                    if k == 3 and c > 0:
                        dve.wait_ge(normed, normed_count(c - 1, 1))
                    if k == 5:
                        dve.wait_ge(normed, normed_count(c, 0))
                        dve.wait_ge(pool_post, pool_count(c, 0) + 1)
                    nc.vector.tensor_tensor(res[:, :, :], ring[:, slot, 0, :].rearrange("p (t d) -> p t d", d=D), added,
                                            ALU.add).then_inc(unit_free, 1)
                    dve.wait_ge(unit_free, 2 + u)
                    for t in range(TPC):
                        nc.vector.bn_stats(stats[:, t, :], res[:, t, :]).then_inc(dve_post, 1)
                    for t in range(TPC):
                        dve.wait_ge(dve_post, at + t)
                        nc.vector.bn_aggr(mv[:, t, :], stats[:, t, :]).then_inc(dve_post, 1)

            def apply_norm(c, norm):
                dve.wait_ge(pool_post, pool_count(c, norm))
                if norm and c > 0:
                    dve.wait_ge(stored, 16 * c)
                for t in range(TPC):
                    nc.vector.tensor_scalar((y_sb if norm else x1)[:, t, :], res[:, t, :], mv[:, t, 0:1], rstd[:, t:t + 1],
                                            ALU.subtract, ALU.mult).then_inc(normed, 1)

            def body(g, part):
                u = 0
                for e in schedule(part):
                    if e[0] in RING_EVENTS:
                        slot = ring_slot(part, u)
                        u += 1
                        n = ring_unit(g, part, u)
                    if e[0] == "P":
                        rotate(e[1])
                    if e == ("P", 1):
                        dve.wait_ge(ld_ffn, 48)
                        nc.vector.tensor_reduce(wst[:, 0:1], ffn_sb[:, :], AX.X, ALU.max, apply_absolute_value=True).then_inc(wq_step, 1)
                    if e[0] == "A":
                        row_max(e[2], e[3], slot, n)
                        if e[3] == score_units(e[2])[-1]:
                            combine(e[2], n)
                    if e[0] == "M":
                        rows(e[2], slot, n)
                    if e[0] == "L":
                        quantise(slot, n)
                    if e[0] == "POST":
                        post(e[1], e[2], slot, n)
                    if e[0] == "NORM":
                        apply_norm(e[1], e[2])

            groups(dve, body)

        @block.tensor
        def _(pe):
            pe.wait_ge(consts, 6)
            pe.wait_ge(ld_w, 48)
            bank = prep_begin(pe, ("W", 0))
            for w in range(3):
                nc.tensor.transpose(bank[:, w * 128:(w + 1) * 128], wqkv_sb[:, w, :], ident[:, :])
            nc.tensor.transpose(bank[:, 384:512], wo_sb[:, :], ident[:, :]).then_inc(bank_done[0], 1)
            bank = prep_begin(pe, ("L", 0))
            nc.tensor.transpose(bank[0:RANK, 0:128], a_sb[:, :], ident[:, :]).then_inc(bank_done[1], 1)

            def transpose_x(c):
                pe.wait_ge(ld_x[c], 16)
                bank = prep_begin(pe, ("X", c))
                for t in range(TPC):
                    last = nc.tensor.transpose(bank[:, t * TOK:(t + 1) * TOK], x_sb[:, c * TPC + t, :], ident[:, :])
                last.then_inc(bank_done[prep_bank_of(("X", c))[0]], 1)

            def prep(c):
                if c == 0:
                    transpose_x(0)
                    pe.wait_ge(w_done, 6)
                b, n = prep_bank_of(("X", c))
                pe.wait_ge(bank_free[b], n)
                for kind, w in (("Q", wT[:, 0, :]), ("QS", wTs[:, 0, :]), ("K", wT[:, 1, :]), ("KS", wTs[:, 1, :])):
                    bank = prep_begin(pe, (kind, c))
                    nc.tensor.matmul(bank, w, xT[:, c % 2, :], start=True, stop=True).then_inc(bank_done[prep_bank_of((kind, c))[0]], 1)
                if c + 1 < NC:
                    transpose_x(c + 1)
                bank = prep_begin(pe, ("V", c))
                for t in range(TPC):
                    last = nc.tensor.matmul(bank[:, t * D:(t + 1) * D], xT[:, c % 2, t * TOK:(t + 1) * TOK],
                                            wT[:, 2, :], start=True, stop=True)
                last.then_inc(bank_done[prep_bank_of(("V", c))[0]], 1)

            def scores(c, unit, slot, u_free):
                kk, ii, hp = unit
                w = CH if kk < c else (ii + 1) * TOK
                pe.wait_ge(unit_free, u_free)
                for i in range(2):
                    h = 2 * hp + i
                    dst = ring[:, slot, i, :]
                    last = nc.tensor.matmul(dst[:, 0:w], qA[:, c, h, ii * TOK:(ii + 1) * TOK], kA[:, kk, h, 0:w],
                                            start=True, stop=kk < c)
                    if kk == c:
                        last = nc.tensor.matmul(dst[:, w - TOK:w], ident_h[:, :], causal[:, :], start=False, stop=True)
                last.then_inc(unit_done, 1)

            def maxima_rows(c, slot, u_free, before, n):
                pe.wait_ge(unit_free, u_free)
                pe.wait_ge(nsplit, before * 4 + 4 * n)
                nc.tensor.transpose(ring[:, slot, 0, 0:TOK // 2].bitcast(bf16), nparts[:, c, :], ident_h[:, :]).then_inc(unit_done, 1)

            def low_rank(slot, u_free):
                pe.wait_ge(unit_free, u_free)
                pe.wait_ge(ld_ffn, 48)
                pe.wait_ge(bank_free[1], 1)
                nc.tensor.matmul(ring[:, slot, 0, 0:D], aT[:, :], b_sb[:, :], start=True, stop=True).then_inc(unit_done, 1)

            def post(c, k, slot, u_free):
                base = DVE_POST * c
                pe.wait_ge(unit_free, u_free)
                if k < 2:
                    pe.wait_ge(o_free, 1 + (NG - 1) * NC + c + 1)
                    for i in range(2):
                        t = c * TPC + 2 * k + i
                        for g in range(NG):
                            last = nc.tensor.transpose(ring[:, slot, i, g * 128:(g + 1) * 128],
                                                       oT[:, g, t * TOK:(t + 1) * TOK], ident[:, :])
                if k == 2:
                    pe.wait_ge(unit_free, u_free + 1)
                    for t in range(TPC):
                        last = nc.tensor.transpose(ring[:, slot, 0, t * TOK:(t + 1) * TOK], on[:, t, :], ident[:, :])
                if k == 3:
                    pe.wait_ge(unit_free, u_free + 1)
                    for t in range(TPC):
                        last = nc.tensor.matmul(ring[:, slot, 0, t * D:(t + 1) * D], onT[:, t * TOK:(t + 1) * TOK],
                                                wT[:, 3, :], start=True, stop=True)
                if k == 4:
                    pe.wait_ge(normed, normed_count(c, 0))
                    for t in range(TPC):
                        last = nc.tensor.transpose(ring[:, slot, 0, t * TOK:(t + 1) * TOK], x1[:, t, :], ident[:, :])
                if k == 5:
                    pe.wait_ge(unit_free, u_free + 1)
                    for t in range(TPC):
                        last = nc.tensor.matmul(ring[:, slot, 0, t * D:(t + 1) * D], x1T[:, t * TOK:(t + 1) * TOK],
                                                ffn_q[:, :], start=True, stop=True)
                last.then_inc(unit_done, 1)

            def body(g, part):
                u, split = 0, 0 if part == "first" else 2
                for e in schedule(part):
                    if e[0] in RING_EVENTS:
                        slot = ring_slot(part, u)
                        u_free = ring_unit(g, part, u + 1)
                        u += 1
                    if e[0] == "P":
                        prep(e[1])
                    if part == "first" and e == ("S", 0, 0, 0):
                        for b in range(4):
                            pe.wait_ge(bank_free[b], (len(PREP) - b + 3) // 4)
                        pe.sem_inc(probs_free, PRING)
                    if e[0] == "L":
                        low_rank(slot, u_free)
                    if e[0] == "A":
                        if e[3] == (0, 0, 0):
                            pe.wait_ge(qkA_in[e[2]], g * 16 * N_A + (1 + e[1]) * 16 * N_A)
                        scores(e[2], e[3], slot, u_free)
                    if e[0] == "M":
                        split += 1
                        maxima_rows(e[2], slot, u_free, g * 4, split)
                    if e[0] == "S":
                        c, j = e[1], e[2]
                        J = step_index(c, j)
                        lo = max(0, j - TPC * c) * TOK
                        if j == 0 and e[3] == 0:
                            pe.wait_ge(qkB_in[c], g * 32 + 32)
                            pe.wait_ge(mrow_in[c], g * 16 + 16)
                        for h in (2 * e[3], 2 * e[3] + 1):
                            n = J * HG + h
                            used = n + 1 if n >= SBANKS else SBANKS if n == 0 else n
                            pe.wait_ge(exp_done, g * BLOCKS + used)
                            nc.tensor.matmul(sT[:, n % SBANKS, lo:CH], kB[:, j // TPC, h, (j % TPC) * TOK:(j % TPC + 1) * TOK],
                                             qB[:, c, h, lo:CH], start=True, stop=True).then_inc(s_done, 1)
                    if e[0] == "PV":
                        c, j = e[1], e[2]
                        J = step_index(c, j)
                        lo = max(0, j - TPC * c) * TOK
                        if j == 0:
                            pe.wait_ge(o_free, g * NC + (c + 1))
                            pe.wait_ge(v_staged, g * NC + (4 + c + 1))
                        if j >= TPC * c:
                            pe.wait_ge(masked, g * (NC * TPC) + (j + 1))
                        else:
                            pe.wait_ge(exp_done, g * BLOCKS + (SBANKS + (J + 1) * HG))
                        for h in range(HG):
                            last_pv = nc.tensor.matmul(oP[VW * h:VW * (h + 1), lo:CH], v_g[:, j, h, :],
                                                       probs[:, J % PRING, h, lo:CH], start=j == 0,
                                                       stop=j == TPC * (c + 1) - 1)
                        last_pv.then_inc(probs_free, 1)
                    if e[0] == "POST":
                        post(e[1], e[2], slot, u_free)

            groups(pe, body)


_INS = ['L0_attn_x', 'L0_attn_W_qkv', 'L0_attn_W_o', 'L0_ffn_kernel', 'L0_ffn_bias', 'L0_ffn_a', 'L0_ffn_b']
_OUTS = [((1, S, D), 'float32')]


def kernel(**inputs):
    import numpy as _np
    import concourse.bacc as _bacc
    from concourse import mybir as _mybir
    from concourse.bass_utils import run_bass_kernel_spmd as _run

    nc = _bacc.Bacc("TRN2", target_bir_lowering=False, num_devices=1)
    arrays, args = {}, []
    for name in _INS:
        a = _np.ascontiguousarray(inputs[name])
        arrays[f"in_{name}_dram"] = a
        args.append(nc.dram_tensor(f"in_{name}_dram", a.shape, _mybir.dt.from_np(a.dtype), kind="ExternalInput").ap())
    tables = rope_tables()
    arrays["rope_tables_dram"] = tables
    args.append(nc.dram_tensor("rope_tables_dram", tables.shape, _mybir.dt.from_np(tables.dtype), kind="ExternalInput").ap())
    for i, (shape, dtype) in enumerate(_OUTS):
        dt = _mybir.dt.from_np(_np.dtype(dtype))
        args.append(nc.dram_tensor(f"out_{i}_dram", shape, dt, kind="ExternalOutput").ap())
    attention_block(nc, *args)
    r = _run(nc, [arrays], core_ids=[0])
    got = tuple(r.results[0][f"out_{i}_dram"] for i in range(len(_OUTS)))
    return got[0]
```
